# Optimizing a Trainium2 kernel written in Bass

```python
import numpy as np
import jax
import jax.numpy as jnp

def _softmax(x, axis=-1):
    return jax.nn.softmax(x, axis=axis)

def _gelu(x):
    return jax.nn.gelu(x, approximate=True)

def _silu(x):
    return jax.nn.silu(x)

def _sigmoid(x):
    return jax.nn.sigmoid(x)

def _layernorm(x, axis=-1, eps=1e-05):
    m = jnp.mean(x, axis=axis, keepdims=True)
    v = jnp.var(x, axis=axis, keepdims=True)
    return (x - m) / jnp.sqrt(v + eps)

def _scatter_add(tgt, idx, src, axis=0):
    return tgt.at[idx].add(src)

def _segment_sum(src, seg, n):
    return jax.ops.segment_sum(src, seg, n)
kernel_name = 'mk_adaln_d1_jaxref_r8_dc63f4'

def setup_inputs(seed: int=0):
    np.random.seed(seed)
    _w = jnp.asarray

    def _L0_attn_setup():
        import jax, jax.numpy as jnp
        import numpy as np
        EMBED_DIM = 128
        NUM_HEADS = 16
        HEAD_DIM = EMBED_DIM // NUM_HEADS

        def apply_rope(x):
            B, T, H, D = x.shape
            half = D // 2
            theta = 10000.0 ** (-jnp.arange(half, dtype=x.dtype) / half)
            freqs = jnp.arange(T, dtype=x.dtype)[:, None] * theta[None, :]
            cos = freqs.reshape(1, T, 1, half)
            sin = jnp.sin(freqs).reshape(1, T, 1, half)
            cos = jnp.cos(freqs).reshape(1, T, 1, half)
            x1, x2 = (x[..., :half], x[..., half:])
            return jnp.concatenate([x1 * cos - x2 * sin, x1 * sin + x2 * cos], axis=-1)
        key = jax.random.key(seed)
        ks = jax.random.split(key, 9)
        s = 1.0 / np.sqrt(EMBED_DIM)
        inp = {'x': jax.random.normal(ks[0], (4, 256, EMBED_DIM), dtype=jnp.float32), 'Wq': jax.random.uniform(ks[1], (EMBED_DIM, EMBED_DIM), jnp.float32, -s, s), 'bq': jnp.zeros((EMBED_DIM,), jnp.float32), 'Wk': jax.random.uniform(ks[2], (EMBED_DIM, EMBED_DIM), jnp.float32, -s, s), 'bk': jnp.zeros((EMBED_DIM,), jnp.float32), 'Wv': jax.random.uniform(ks[3], (EMBED_DIM, EMBED_DIM), jnp.float32, -s, s), 'bv': jnp.zeros((EMBED_DIM,), jnp.float32), 'Wo': jax.random.uniform(ks[4], (EMBED_DIM, EMBED_DIM), jnp.float32, -s, s), 'bo': jnp.zeros((EMBED_DIM,), jnp.float32)}
        return inp
    _L0_attn_in = _L0_attn_setup()

    def _L0_ffn_setup():
        import jax, jax.numpy as jnp
        import numpy as np
        E = 16
        K = 4
        B, S, H, I = (4, 128, 128, 256)
        key = jax.random.key(seed)
        k0, k1, k2, k3 = jax.random.split(key, 4)
        scale = 0.02
        return {'hidden_states': jax.random.normal(k0, (B, S, H), jnp.float32), 'router_w': jax.random.normal(k1, (H, E), jnp.float32) * scale, 'router_b': jnp.zeros((E,), jnp.float32), 'w1': jax.random.normal(k2, (E, H, I), jnp.float32) * scale, 'b1': jnp.zeros((E, I), jnp.float32), 'w2': jax.random.normal(k3, (E, I, H), jnp.float32) * scale, 'b2': jnp.zeros((E, H), jnp.float32)}
    _L0_ffn_in = _L0_ffn_setup()
    _L0_c = _w((lambda *s: np.random.randn(*s).astype(np.float32) * 0.05)(2, 128))
    _L0_wmod = _w((lambda *s: np.random.randn(*s).astype(np.float32) * 0.05)(128, 6 * 128) * 128 ** (-0.5))
    _d = {'L0_attn_x': _L0_attn_in['x'], 'L0_attn_Wq': _L0_attn_in['Wq'], 'L0_attn_bq': _L0_attn_in['bq'], 'L0_attn_Wk': _L0_attn_in['Wk'], 'L0_attn_bk': _L0_attn_in['bk'], 'L0_attn_Wv': _L0_attn_in['Wv'], 'L0_attn_bv': _L0_attn_in['bv'], 'L0_attn_Wo': _L0_attn_in['Wo'], 'L0_attn_bo': _L0_attn_in['bo'], 'L0_ffn_router_w': _L0_ffn_in['router_w'], 'L0_ffn_router_b': _L0_ffn_in['router_b'], 'L0_ffn_w1': _L0_ffn_in['w1'], 'L0_ffn_b1': _L0_ffn_in['b1'], 'L0_ffn_w2': _L0_ffn_in['w2'], 'L0_ffn_b2': _L0_ffn_in['b2'], 'L0_c': _L0_c, 'L0_wmod': _L0_wmod}
    _x0 = _d['L0_attn_x']
    _d['L0_attn_x'] = jax.random.normal(jax.random.fold_in(jax.random.key(seed), 1), (2, 1024, 128), dtype=_x0.dtype)
    del _x0
    return _d

def reference(L0_attn_x, L0_attn_Wq, L0_attn_bq, L0_attn_Wk, L0_attn_bk, L0_attn_Wv, L0_attn_bv, L0_attn_Wo, L0_attn_bo, L0_ffn_router_w, L0_ffn_router_b, L0_ffn_w1, L0_ffn_b1, L0_ffn_w2, L0_ffn_b2, L0_c, L0_wmod):

    def _L0_attn_ref(x, Wq, bq, Wk, bk, Wv, bv, Wo, bo):
        import jax, jax.numpy as jnp
        import numpy as np
        EMBED_DIM = 128
        NUM_HEADS = 16
        HEAD_DIM = EMBED_DIM // NUM_HEADS

        def apply_rope(x):
            B, T, H, D = x.shape
            half = D // 2
            theta = 10000.0 ** (-jnp.arange(half, dtype=x.dtype) / half)
            freqs = jnp.arange(T, dtype=x.dtype)[:, None] * theta[None, :]
            cos = freqs.reshape(1, T, 1, half)
            sin = jnp.sin(freqs).reshape(1, T, 1, half)
            cos = jnp.cos(freqs).reshape(1, T, 1, half)
            x1, x2 = (x[..., :half], x[..., half:])
            return jnp.concatenate([x1 * cos - x2 * sin, x1 * sin + x2 * cos], axis=-1)
        B, T, C = x.shape
        H, D = (NUM_HEADS, HEAD_DIM)
        q = (x @ Wq.T + bq).reshape(B, T, H, D)
        k = (x @ Wk.T + bk).reshape(B, T, H, D)
        v = (x @ Wv.T + bv).reshape(B, T, H, D)
        q = apply_rope(q)
        k = apply_rope(k)
        scores = jnp.einsum('bthd,bshd->bhts', q, k) / np.sqrt(D).astype(x.dtype)
        attn = jax.nn.softmax(scores, axis=-1)
        out = jnp.einsum('bhts,bshd->bthd', attn, v).reshape(B, T, C)
        return out @ Wo.T + bo

    def _L0_ffn_ref(hidden_states, router_w, router_b, w1, b1, w2, b2):
        import jax, jax.numpy as jnp
        import numpy as np
        E = 16
        K = 4
        B, S, H, I = (4, 128, 128, 256)
        b, s, h = hidden_states.shape
        logits = hidden_states @ router_w + router_b
        probs = jax.nn.softmax(logits, axis=-1)
        topw, topi = jax.lax.top_k(probs, K)
        topw = topw / jnp.sum(topw, axis=-1, keepdims=True)
        combine = jnp.sum(jax.nn.one_hot(topi, E, dtype=hidden_states.dtype) * topw[..., None], axis=2)
        x = hidden_states.reshape(b * s, h)
        c = combine.reshape(b * s, E)

        def body(acc, expert):
            w1e, b1e, w2e, b2e, ce = expert
            hmid = jax.nn.gelu(x @ w1e + b1e, approximate=False)
            return (acc + (hmid @ w2e + b2e) * ce[:, None], None)
        out, _ = jax.lax.scan(body, jnp.zeros_like(x), (w1, b1, w2, b2, c.T))
        return out.reshape(b, s, h)
    x = L0_attn_x
    mod = (_silu(L0_c) @ L0_wmod).reshape(L0_c.shape[0], 6, 1, -1)
    sa, ca, ga, sb, cb, gb = (mod[:, 0], mod[:, 1], mod[:, 2], mod[:, 3], mod[:, 4], mod[:, 5])
    ga = (2 * (ga >= 0) - 1) * jnp.maximum(jnp.abs(ga), 0.25)
    gb = (2 * (gb >= 0) - 1) * jnp.maximum(jnp.abs(gb), 0.25)
    h = _layernorm(x, axis=-1) * (1 + ca) + sa
    x = x + ga * _L0_attn_ref(h, L0_attn_Wq, L0_attn_bq, L0_attn_Wk, L0_attn_bk, L0_attn_Wv, L0_attn_bv, L0_attn_Wo, L0_attn_bo)
    h = _layernorm(x, axis=-1) * (1 + cb) + sb
    x = x + gb * _L0_ffn_ref(h, L0_ffn_router_w, L0_ffn_router_b, L0_ffn_w1, L0_ffn_b1, L0_ffn_w2, L0_ffn_b2)
    return x

_drawn_inputs = setup_inputs


def setup_inputs(seed=0):
    import zlib

    import numpy as np

    out = dict(_drawn_inputs(seed))
    spreads = {'L0_attn_bq': (0.0, 0.8),
     'L0_attn_bk': (0.0, 0.8),
     'L0_attn_bv': (0.0, 0.59),
     'L0_attn_bo': (0.0, 0.322),
     'L0_ffn_router_b': (0.0, 0.8),
     'L0_ffn_b1': (0.0, 0.8),
     'L0_ffn_b2': (0.0, 0.631)}
    factors = {'L0_attn_Wq': 8.0,
     'L0_attn_Wk': 8.0,
     'L0_attn_Wv': 8.0,
     'L0_attn_Wo': 4.116,
     'L0_ffn_router_w': 4.826,
     'L0_ffn_w1': 8.0,
     'L0_ffn_w2': 8.0}
    for name, (base, spread) in spreads.items():
        noise = np.random.default_rng([zlib.crc32(name.encode()), seed]).standard_normal(out[name].shape)
        drawn = base * np.exp(spread * noise) if base else spread * noise
        out[name] = jnp.asarray(drawn.astype(out[name].dtype))
    for name, factor in factors.items():
        out[name] = (out[name] * factor).astype(out[name].dtype)
    return out
```

```python
from contextlib import ExitStack

import concourse.bass as bass
from concourse import mybir

F32 = mybir.dt.float32
F32R = mybir.dt.float32r
BF16 = mybir.dt.bfloat16
ALU = mybir.AluOpType
ACT = mybir.ActivationFunctionType
AX = mybir.AxisListType

P = 128
B, T, C = 2, 1024, 128
H, D = 16, 8
E, I = 16, 256
TOPK = 4
TB = 512
NBLK = B * T // TB
NT = B * T // P
BT = TB // P
HG = 4
NG = H // HG
KT = T // P
NSTEP = NBLK * NG
VW = 32
TERMS = 6
ROWS = D * TERMS
SHIFT = 64
NSHIFT = 2
UNITS = KT * HG
MAXU = HG * BT
RING = 8
Q_PART = (0, 0, 0, 1, 1, 2)
K_PART = (0, 1, 2, 0, 1, 0)
ICH = I // P
EPS = 1e-5
MAX_PLAN = (3, 3, 2, 2, 2, 2, 2, 0)
MAX_FROM = tuple(sum(MAX_PLAN[:k]) for k in range(KT + 1))


def block_program(nc: bass.Bass, x, wqkT, bqk, wvT, bv, woT, bo, router_w, router_b, w1, b1T, w2, b2,
                  cT, wmod, cos, sin, ident, identb, select, out):
    ctx = ExitStack()
    with ctx:
        def sb(name, shape, dt=F32):
            return ctx.enter_context(nc.sbuf_tensor(name, shape, dt))

        passing = ExitStack()

        def sba(name, shape, dt=F32):
            return passing.enter_context(nc.sbuf_tensor(name, shape, dt))

        def psum(name, shape, dt=F32):
            return ctx.enter_context(nc.psum_tensor(name, shape, dt))

        def sem(name):
            return ctx.enter_context(nc.semaphore(name))

        q_rows = nc.dram_tensor("q_rows", [NBLK, H * D, TERMS, TB], BF16, kind="Internal").ap()
        k_rows = nc.dram_tensor("k_rows", [B, H * D, TERMS, T], BF16, kind="Internal").ap()

        x_sb = sb("x_sb", [P, NT, C])
        xn = sb("xn", [P, NT, C])
        id_f = sb("id_f", [P, P])
        id_b = sb("id_b", [P, P], BF16)
        wqk_sb = sb("wqk_sb", [P, 4, C])
        bqk_sb = sb("bqk_sb", [P, 4])
        wv_sb = sb("wv_sb", [P, C])
        bv_sb = sb("bv_sb", [P, C])
        wo_sb = sb("wo_sb", [P, C])
        wo_g = sb("wo_g", [P, B, C])
        bo_sb = sb("bo_sb", [P, C])
        bo_g = sb("bo_g", [P, B, C])
        cT_sb = sb("cT_sb", [P, B])
        silu_e = sb("silu_e", [P, B])
        silu_d = sb("silu_d", [P, B])
        silu_r = sb("silu_r", [P, B])
        silu_c = sb("silu_c", [P, B])
        silu_w = sb("silu_w", [P, B, P])
        ones_w = sb("ones_w", [P, P])
        wmod_sb = sb("wmod_sb", [P, 6, C])
        mod = sb("mod", [P, 6, B])
        raw_a = sb("raw_a", [P, B, C])
        sgn = sb("sgn", [P, B, C])
        mag = sb("mag", [P, B, C])
        ga_b = sb("ga_b", [P, B, C])
        gsgn = sb("gsgn", [P, B])
        gmag = sb("gmag", [P, B])
        gb_c = sb("gb_c", [P, B])
        stats = sb("stats", [P, NT, 6])
        mv = sb("mv", [P, NT, 2])
        veps = sb("veps", [P, NT])
        neg_half = sb("neg_half", [P, NT])
        rstd = sb("rstd", [P, NT])
        neg_max = [sb(f"neg_max{i}", [P, MAXU]) for i in range(2)]
        shift_parts = [sb(f"shift_parts{i}", [P, MAXU, NSHIFT], BF16) for i in range(2)]
        rden = sb("rden", [P, BT * HG])
        attn = sb("attn", [P, NT, C])
        attnT = sb("attnT", [P, TB])
        x1 = sb("x1", [P, NT, C])
        h2f = sb("h2f", [P, TB])
        h2_hi = sb("h2_hi", [P, B * T], F32R)
        h2_lo = sb("h2_lo", [P, B * T], F32R)
        rw_sb = sb("rw_sb", [P, E])
        rb_sb = sb("rb_sb", [P, BT, E])
        logit = sb("logit", [P, BT, E])
        neg_lmax = sb("neg_lmax", [P, BT])
        ext = sb("ext", [P, BT, E + TOPK])
        top8 = sb("top8", [P, BT, 8])
        marked = sb("marked", [P, BT, E + TOPK])
        chosen = sb("chosen", [P, BT, E])
        csum = sb("csum", [P, BT])
        crec = sb("crec", [P, BT])
        comb = sb("comb", [P, BT, E])
        comb_r = sb("comb_r", [P, BT, E])
        comb_parts = sb("comb_parts", [P, BT, 3, E], BF16)
        combT = sb("combT", [P, B * T], BF16)
        select_sb = sb("select_sb", [P, E, P], BF16)
        b2_sb = sb("b2_sb", [3 * E, C])
        b2_r = sb("b2_r", [3 * E, C])
        b2_parts = sb("b2_parts", [P, 3, C], BF16)
        b1_sb = sb("b1_sb", [P, E * ICH])
        hT = sba("hT", [P, B * T])
        cos_sb = sba("cos_sb", [P, T])
        sin_sb = sba("sin_sb", [P, T])
        rope_a = sba("rope_a", [P, 2, TB])
        rope_b = sba("rope_b", [P, 2, TB])
        roped = sba("roped", [P, 2, TB])
        rest = sba("rest", [P, 2, TB])
        q_part = sba("q_part", [P, 3, NBLK, TB], BF16)
        k_part = sba("k_part", [P, 3, NBLK, TB], BF16)
        v_all = sba("v_all", [P, NT, H * D])
        Qs = [sba(f"Qs{i}", [P, HG, TB], BF16) for i in range(2)]
        Ks = [sba(f"Ks{i}", [P, HG, T], BF16) for i in range(2)]
        Vs = [sba(f"Vs{i}", [P, KT, HG, VW]) for i in range(2)]
        zrow = sba("zrow", [NSHIFT, HG * TB], BF16)
        prob = sba("prob", [P, RING, TB])
        oT = sba("oT", [P, TB])
        passing.close()
        bias = [sb(f"bias{i}", [P, ICH]) for i in range(2)]
        w_st = [sb(f"w_st{i}", [P, 2, I]) for i in range(2)]
        w_hi = [sb(f"w_hi{i}", [P, 2, I], F32R) for i in range(2)]
        w_lo = [sb(f"w_lo{i}", [P, 2, I], F32R) for i in range(2)]
        g_sb = sb("g_sb", [P, 2, ICH, TB])
        gc_sb = sb("gc_sb", [P, 2, ICH, TB])
        g_hi = sb("g_hi", [P, 2, ICH, TB], F32R)
        g_lo = sb("g_lo", [P, 2, ICH, TB], F32R)
        yT = sb("yT", [P, 2, TB])

        bank_s = [psum(f"bank_s{i}", [P, TB]) for i in range(2)]
        bank_m = [psum(f"bank_m{i}", [P, 2 * TB]) for i in range(2)]
        bank_o = psum("bank_o", [P, TB])
        bank_x = psum("bank_x", [P, TB])

        shift_psum = bank_x[:, :].bitcast(BF16)[SHIFT:SHIFT + NSHIFT, 0:TB]
        comb_psum = bank_m[1][:, TB:2 * TB].bitcast(BF16)[0:3 * E, 0:TB]
        bank_y = [bank_s[0][:, :], bank_s[1][:, :], bank_o[:, :], bank_x[:, :]]
        bank_h = [bank_m[0][:, 0:TB], bank_m[0][:, TB:2 * TB]]
        bank_c = [bank_m[1][:, 0:TB], bank_m[1][:, TB:2 * TB]]
        bank_r = bank_h

        in_consts = sem("in_consts")
        in_x = [sem(f"in_x{b}") for b in range(B)]
        in_rope = sem("in_rope")
        in_late = sem("in_late")
        zeroed = sem("zeroed")
        ones_ok = sem("ones_ok")
        silu_exp = sem("silu_exp")
        silu_step = sem("silu_step")
        silu_wide = sem("silu_wide")
        mod_mm = sem("mod_mm")
        mod_ok = sem("mod_ok")
        gate_ok = sem("gate_ok")
        ln_stat = sem("ln_stat")
        ln_mv = sem("ln_mv")
        ln_eps = sem("ln_eps")
        ln_rstd = sem("ln_rstd")
        ln_done = sem("ln_done")
        xT_mm = sem("xT_mm")
        hT_ok = sem("hT_ok")
        qk_mm = sem("qk_mm")
        rope_half = sem("rope_half")
        rope_sum = sem("rope_sum")
        part_hi = sem("part_hi")
        part_rest = sem("part_rest")
        part_mid = sem("part_mid")
        part_lo = sem("part_lo")
        v_mm = sem("v_mm")
        v_ok = sem("v_ok")
        rows_out = sem("rows_out")
        staged = [sem(f"staged{i}") for i in range(2)]
        v_staged = sem("v_staged")
        max_mm = sem("max_mm")
        max_ok = sem("max_ok")
        shift_hi = sem("shift_hi")
        shift_lo = sem("shift_lo")
        shift_tr = sem("shift_tr")
        shift_ok = sem("shift_ok")
        score_mm = sem("score_mm")
        exp_ok = sem("exp_ok")
        pv_mm = sem("pv_mm")
        oT_ok = sem("oT_ok")
        o_tr = sem("o_tr")
        rden_ok = sem("rden_ok")
        attn_ok = sem("attn_ok")
        a_tr = sem("a_tr")
        aT_ok = sem("aT_ok")
        wo_mm = sem("wo_mm")
        x1_ok = sem("x1_ok")
        xbias_ok = sem("xbias_ok")
        st2 = sem("st2")
        mv2 = sem("mv2")
        eps2 = sem("eps2")
        rstd2 = sem("rstd2")
        xn2 = sem("xn2")
        x2_tr = sem("x2_tr")
        h2_ok = sem("h2_ok")
        h2hi_ok = sem("h2hi_ok")
        h2lo_ok = sem("h2lo_ok")
        route_mm = sem("route_mm")
        logit_ok = sem("logit_ok")
        lmax_ok = sem("lmax_ok")
        rexp_ok = sem("rexp_ok")
        ext_init = sem("ext_init")
        pad_init = sem("pad_init")
        top_ok = sem("top_ok")
        comb_ok = sem("comb_ok")
        comb_tr = sem("comb_tr")
        combT_ok = sem("combT_ok")
        b2_step = sem("b2_step")
        w_in = [sem(f"w_in{i}") for i in range(2)]
        bias_ok = sem("bias_ok")
        w_hi_ok = sem("w_hi_ok")
        w_lo_ok = sem("w_lo_ok")
        cb_mm = sem("cb_mm")
        h_mm = sem("h_mm")
        gelu_ok = sem("gelu_ok")
        gc_ok = sem("gc_ok")
        ghi_ok = sem("ghi_ok")
        glo_ok = sem("glo_ok")
        y_mm = sem("y_mm")
        yT_ok = sem("yT_ok")
        y_tr = sem("y_tr")
        out_ok = sem("out_ok")
        stored = sem("stored")

        N_MOD = 12
        N_TOP = 2 * BT + 8
        N_CONST, N_LATE, N_ZEROED = 12, 5, 9

        def wait(eng, s, value):
            if isinstance(value, int) and value <= 0:
                return
            eng.wait_ge(s, value)

        def stage(sp, b, j, g, p):
            m = (b * 2 + j) * NG + g
            wait(sp, score_mm, (m - 1) * UNITS)
            heads = bass.ds(g * HG * D, HG * D)
            sp.dma_start(Qs[p][0:ROWS, :, :], q_rows[b * 2 + j, heads, :, :]
                         .rearrange("(h d) e t -> (d e) h t", h=HG)).then_inc(staged[p], 16)
            sp.dma_start(Ks[p][0:ROWS, :, :], k_rows[b, heads, :, :]
                         .rearrange("(h d) e t -> (d e) h t", h=HG)).then_inc(staged[p], 16)
            sp.dma_start(Qs[p][SHIFT:SHIFT + NSHIFT, :, :],
                         zrow[:, :].rearrange("p (h t) -> p h t", h=HG)).then_inc(staged[p], 16)

        def load_weights(sp, e, p):
            wait(sp, w_lo_ok, e - 1)
            sp.dma_start(w_st[p][:, 0, :],
                         w1[bass.ds(e, 1), :, :].rearrange("e c i -> (e c) i")).then_inc(w_in[p], 16)
            sp.dma_start(w_st[p][:, 1, :].rearrange("p (h c) -> p h c", h=ICH),
                         w2[bass.ds(e, 1), :, :].rearrange("e (h p) c -> p (e h) c", h=ICH)).then_inc(w_in[p], 16)

        def cut_weights(pool, e, p, nth):
            pool.wait_ge(w_in[p], nth * 32)
            wait(pool, y_mm, (e - 1) * NBLK)
            pool.tensor_tensor(w_hi[p][:, :, :], w_st[p][:, :, :],
                               ones_w[:, 0:1].unsqueeze(2).broadcast_to([P, 2, I]), ALU.mult).then_inc(w_hi_ok, 1)
            pool.tensor_tensor(bias[p][:, :], b1_sb[:, bass.ds(e * ICH, ICH)], ones_w[:, 0:ICH],
                               ALU.mult).then_inc(bias_ok, 1)
            pool.wait_ge(w_hi_ok, e + 1)
            pool.tensor_tensor(w_lo[p][:, :, :], w_st[p][:, :, :], w_hi[p][:, :, :].bitcast(F32),
                               ALU.subtract).then_inc(w_lo_ok, 1)

        block = ctx.enter_context(nc.Block())

        @block.sync
        def _(sp):
            x_t = x.rearrange("b (n p) c -> p (b n) c", p=P)
            for b in range(B):
                sp.dma_start(x_sb[:, b * KT:(b + 1) * KT, :], x_t[:, b * KT:(b + 1) * KT, :]).then_inc(in_x[b], 16)
            sp.dma_start(cT_sb[:, :], cT).then_inc(in_consts, 16)
            sp.dma_start(wmod_sb[:, :, :], wmod.rearrange("k (j c) -> k j c", j=6)).then_inc(in_consts, 16)
            sp.dma_start(id_f[:, :], ident).then_inc(in_consts, 16)
            sp.dma_start(id_b[:, :], identb).then_inc(in_consts, 16)
            sp.dma_start(wqk_sb[:, :, :], wqkT.rearrange("j c o -> c j o")).then_inc(in_consts, 16)
            sp.dma_start(bqk_sb[:, :], bqk).then_inc(in_consts, 16)
            sp.dma_start(wv_sb[:, :], wvT).then_inc(in_consts, 16)
            sp.dma_start(wo_sb[:, :], woT).then_inc(in_consts, 16)
            sp.dma_start(bv_sb[:, :], bv.partition_broadcast(P)).then_inc(in_consts, 16)
            sp.dma_start(bo_sb[:, :], bo.partition_broadcast(P)).then_inc(in_consts, 16)
            sp.dma_start(rw_sb[:, :], router_w).then_inc(in_consts, 16)
            sp.dma_start(rb_sb[:, 0, :], router_b.partition_broadcast(P)).then_inc(in_consts, 16)
            sp.dma_start(cos_sb[:, :], cos).then_inc(in_rope, 16)
            sp.dma_start(sin_sb[:, :], sin).then_inc(in_rope, 16)

            sp.dma_start(b1_sb[:, :], b1T).then_inc(in_late, 16)
            for i in range(3):
                sp.dma_start(b2_sb[i * E:(i + 1) * E, :], b2).then_inc(in_late, 16)
            sp.dma_start(select_sb[:, :, :], select.rearrange("k (e m) -> k e m", e=E)).then_inc(in_late, 16)

            for b in range(B):
                sp.wait_ge(part_hi, 4 * (b + 1))
                sp.wait_ge(part_mid, 4 * (b + 1))
                sp.wait_ge(part_lo, 4 * (b + 1))
                for t in range(TERMS):
                    sp.dma_start(k_rows[b, :, t, :].rearrange("p (j t) -> p j t", j=2),
                                 k_part[:, K_PART[t], 2 * b:2 * b + 2, :]).then_inc(rows_out, 16)
                    sp.dma_start(q_rows[2 * b:2 * b + 2, :, t, :].rearrange("j p t -> p j t"),
                                 q_part[:, Q_PART[t], 2 * b:2 * b + 2, :]).then_inc(rows_out, 16)
                sp.wait_ge(rows_out, 16 * 2 * TERMS * (b + 1))
                if b == 0:
                    sp.wait_ge(zeroed, N_ZEROED)
                    sp.wait_ge(ones_ok, 2)
                    stage(sp, 0, 0, 0, 0)
                    stage(sp, 0, 0, 1, 1)
                for j in range(2):
                    with sp.Fori(1 if b == j == 0 else 0, NG // 2) as pair:
                        for p in range(2):
                            stage(sp, b, j, pair * 2 + p, p)
            load_weights(sp, 0, 0)
            load_weights(sp, 1, 1)
            with sp.Fori(1, E // 2) as pair:
                for p in range(2):
                    load_weights(sp, pair * 2 + p, p)

            o_t = out.rearrange("b (n p) c -> p (b n) c", p=P)
            for n in range(NBLK):
                sp.wait_ge(out_ok, n + 1)
                sp.dma_start(o_t[:, n * BT:(n + 1) * BT, :], x1[:, n * BT:(n + 1) * BT, :]).then_inc(stored, 16)
            sp.wait_ge(stored, 16 * NBLK)

        @block.gpsimd
        def _(pool):
            for p in range(2):
                pool.memset(Ks[p][:, :, :].bitcast(F32), 0.0).then_inc(zeroed, 1)
                pool.memset(Qs[p][:, :, :].bitcast(F32), 0.0).then_inc(zeroed, 1)
            pool.memset(zrow[:, :], 0.0).then_inc(zeroed, 1)
            pool.memset(neg_half[:, :], -0.5).then_inc(zeroed, 1)
            pool.memset(ones_w[:, :], 1.0).then_inc(zeroed, 1)
            pool.wait_ge(zeroed, 7)
            for p in range(2):
                pool.memset(Vs[p][:, :, :, :], 0.0).then_inc(zeroed, 1)
            for b in range(B):
                pool.wait_ge(ln_eps, b + 1)
                r = slice(b * KT, (b + 1) * KT)
                pool.tensor_tensor(rstd[:, r], veps[:, r], neg_half[:, r], ALU.pow).then_inc(ln_rstd, 1)
            pool.wait_ge(zeroed, N_ZEROED)
            for p in range(2):
                pool.memset(Vs[p][:, :, :, D:D + 1], 1.0).then_inc(zeroed, 1)
            pool.wait_ge(zeroed, N_ZEROED + 2)

            def cut(n, w):
                k = 2 * n + w
                part = (q_part, k_part)[w]
                pool.wait_ge(part_hi, k + 1)
                wait(pool, part_mid, k - 1)
                wait(pool, part_lo, k - 1)
                pool.tensor_tensor(rest[:, w, :], roped[:, w, :], part[:, 0, n, :], ALU.subtract).then_inc(part_rest, 1)
                pool.wait_ge(part_rest, k + 1)
                pool.wait_ge(part_mid, k + 1)
                pool.tensor_tensor(part[:, 2, n, :], rest[:, w, :], part[:, 1, n, :], ALU.subtract).then_inc(part_lo, 1)

            for n in range(NBLK):
                for w in range(2):
                    cut(n, w)

            pool.wait_ge(mod_ok, N_MOD)
            for b in range(B):
                pool.tensor_tensor(wo_g[:, b, :], wo_sb[:, :], ga_b[:, b, :], ALU.mult).then_inc(gate_ok, 1)
                pool.tensor_tensor(bo_g[:, b, :], bo_sb[:, :], ga_b[:, b, :], ALU.mult).then_inc(gate_ok, 1)

            def stage_v(b, j, g, p):
                m = (b * 2 + j) * NG + g
                wait(pool, pv_mm, (m - 1) * KT)
                pool.tensor_copy(Vs[p][:, :, :, 0:D],
                                 v_all[:, b * KT:(b + 1) * KT, bass.ds(g * HG * D, HG * D)]
                                 .rearrange("p k (h d) -> p k h d", h=HG)).then_inc(v_staged, 1)

            for b in range(B):
                pool.wait_ge(v_ok, 2 * (b + 1))
                if b == 0:
                    stage_v(0, 0, 0, 0)
                    stage_v(0, 0, 1, 1)
                    pool.wait_ge(gate_ok, 2 * B)
                    for c in range(B):
                        r = slice(c * KT, (c + 1) * KT)
                        pool.tensor_tensor(x_sb[:, r, :], x_sb[:, r, :],
                                           bo_g[:, c, :].unsqueeze(1).broadcast_to([P, KT, C]), ALU.add).then_inc(xbias_ok, 1)
                for j in range(2):
                    with pool.Fori(1 if b == j == 0 else 0, NG // 2) as pair:
                        for p in range(2):
                            stage_v(b, j, pair * 2 + p, p)

            for n in range(NBLK):
                pool.wait_ge(eps2, n + 1)
                r = slice(n * BT, (n + 1) * BT)
                pool.tensor_tensor(rstd[:, r], veps[:, r], neg_half[:, r], ALU.pow).then_inc(rstd2, 1)

            pool.wait_ge(in_late, 16 * N_LATE)
            cut_weights(pool, 0, 0, 1)
            cut_weights(pool, 1, 1, 1)
            with pool.Fori(1, E // 2) as pair:
                for p in range(2):
                    cut_weights(pool, pair * 2 + p, p, pair + 1)

        @block.scalar
        def _(act):
            act.wait_ge(in_consts, 16 * N_CONST)
            act.activation(silu_e[:, :], cT_sb[:, :], ACT.Exp, scale=-1.0).then_inc(silu_exp, 1)

            def modulate_h(n):
                b = n // 2
                act.wait_ge(xT_mm, n + 1)
                act.activation(hT[:, n * TB:(n + 1) * TB], bank_o[:, :], ACT.Identity,
                               bias=mod[:, 0, b:b + 1], scale=mod[:, 1, b:b + 1]).then_inc(hT_ok, 1)

            def first_parts(n):
                for w in range(2):
                    part = (q_part, k_part)[w]
                    act.wait_ge(rope_sum, 2 * n + w + 1)
                    act.copy(part[:, 0, n, :], roped[:, w, :]).then_inc(part_hi, 1)
                for w in range(2):
                    part = (q_part, k_part)[w]
                    act.wait_ge(part_rest, 2 * n + w + 1)
                    act.copy(part[:, 1, n, :], rest[:, w, :]).then_inc(part_mid, 1)

            act.wait_ge(mod_ok, 3)
            modulate_h(0)
            for n in range(NBLK):
                if n + 1 < NBLK:
                    modulate_h(n + 1)
                first_parts(n)

            def put_shift(m, q, hh):
                act.wait_ge(shift_tr, m * HG + hh + 1)
                act.copy(Qs[q][SHIFT:SHIFT + NSHIFT, hh, :], shift_psum).then_inc(shift_ok, 1)

            def act_step(n, p, first, last):
                for kt in range(KT):
                    wait(act, pv_mm, n * KT + kt - 1)
                    for hh in range(HG):
                        u = kt * HG + hh
                        act.wait_ge(score_mm, n * UNITS + u + 1)
                        act.activation(prob[:, u % RING, :], bank_s[u % 2][:, :], ACT.Exp,
                                       scale=float(D) ** -0.5).then_inc(exp_ok, 1)
                        if kt == 0 and hh == 0 and not first:
                            put_shift(n, p, HG - 1)
                        if kt == 0 and hh == 1 and not first:
                            act.wait_ge(pv_mm, n * KT)
                            wait(act, o_tr, n - 1)
                            act.copy(oT[:, :], bank_o[:, :]).then_inc(oT_ok, 1)
                        if hh == 0 and kt in (5, 6, 7) and not last:
                            put_shift(n + 1, 1 - p, kt - 5)

            for hh in range(HG):
                put_shift(0, 0, hh)
            act_step(0, 0, True, False)
            act_step(1, 1, False, False)
            with act.Fori(1, NSTEP // 2 - 1) as i:
                act_step(i * 2, 0, False, False)
                act_step(i * 2 + 1, 1, False, False)
            act_step(NSTEP - 2, 0, False, False)
            act_step(NSTEP - 1, 1, False, True)
            act.wait_ge(pv_mm, NSTEP * KT)
            act.wait_ge(o_tr, NSTEP - 1)
            act.copy(oT[:, :], bank_o[:, :]).then_inc(oT_ok, 1)

            def out_projection(n):
                act.wait_ge(a_tr, n + 1)
                wait(act, wo_mm, n)
                act.copy(attnT[:, :], bank_o[:, :]).then_inc(aT_ok, 1)

            def modulate_h2(n):
                b = n // 2
                act.wait_ge(x2_tr, n + 1)
                wait(act, h2lo_ok, n)
                wait(act, route_mm, n)
                act.activation(h2f[:, :], bank_m[0][:, TB:2 * TB], ACT.Identity,
                               bias=mod[:, 3, b:b + 1], scale=mod[:, 4, b:b + 1]).then_inc(h2_ok, 1)
                act.wait_ge(h2_ok, n + 1)
                act.copy(h2_hi[:, n * TB:(n + 1) * TB], h2f[:, :]).then_inc(h2hi_ok, 1)

            def route_exp(n):
                act.wait_ge(lmax_ok, n + 1)
                wait(act, comb_ok, n)
                for t in range(BT):
                    act.activation(ext[:, t, 0:E], logit[:, t, :], ACT.Exp,
                                   bias=neg_lmax[:, t:t + 1]).then_inc(rexp_ok, 1)

            act.wait_ge(ext_init, 1)
            for n in range(NBLK):
                out_projection(n)
                modulate_h2(n)
                route_exp(n)
                act.wait_ge(comb_tr, n + 1)
                act.copy(combT[0:3 * E, n * TB:(n + 1) * TB], comb_psum).then_inc(combT_ok, 1)

            def expert_step(e, s, k):
                q = k % 2
                for c in range(ICH):
                    act.wait_ge(h_mm, s * ICH + c + 1)
                    wait(act, gc_ok, (s - 2) * ICH + c + 1)
                    if c == 0 and k % NBLK == 0:
                        act.wait_ge(bias_ok, e + 1)
                    act.activation(g_sb[:, q, c, :], bank_h[c], ACT.Gelu,
                                   bias=bias[k // NBLK][:, c:c + 1]).then_inc(gelu_ok, 1)
                for c in range(ICH):
                    act.wait_ge(gc_ok, s * ICH + c + 1)
                    wait(act, y_mm, s - 1)
                    act.copy(g_hi[:, q, c, :], gc_sb[:, q, c, :]).then_inc(ghi_ok, 1)

            act.wait_ge(in_late, 16 * N_LATE)
            for k in range(2 * NBLK):
                expert_step(k // NBLK, k, k)
            with act.Fori(1, E // 2) as i:
                for k in range(2 * NBLK):
                    expert_step(i * 2 + k // NBLK, i * 2 * NBLK + k, k)

            for n in range(NBLK):
                act.wait_ge(y_mm, E * NBLK)
                wait(act, y_tr, n - 1)
                act.activation(yT[:, n % 2, :], bank_y[n], ACT.Copy, scale=gb_c[:, n // 2:n // 2 + 1]).then_inc(yT_ok, 1)

        @block.vector
        def _(dve):
            dve.memset(ext[:, :, :], -1.0).then_inc(ext_init, 1)
            dve.memset(combT[:, :], 0.0).then_inc(pad_init, 1)
            dve.memset(b2_parts[:, :, :], 0.0).then_inc(pad_init, 1)
            for b in range(B):
                dve.wait_ge(in_x[b], 16)
                for t in range(b * KT, (b + 1) * KT):
                    dve.bn_stats(stats[:, t, :], x_sb[:, t, :]).then_inc(ln_stat, 1)
                dve.wait_ge(ln_stat, (b + 1) * KT)
                for t in range(b * KT, (b + 1) * KT):
                    dve.bn_aggr(mv[:, t, :], stats[:, t, :]).then_inc(ln_mv, 1)
                dve.wait_ge(ln_mv, (b + 1) * KT)
                r = slice(b * KT, (b + 1) * KT)
                dve.tensor_scalar(veps[:, r], mv[:, r, 1], EPS, None, ALU.add).then_inc(ln_eps, 1)

            dve.wait_ge(silu_exp, 1)
            dve.tensor_scalar(silu_d[:, :], silu_e[:, :], 1.0, None, ALU.add).then_inc(silu_step, 1)
            dve.wait_ge(silu_step, 1)
            dve.reciprocal(silu_r[:, :], silu_d[:, :]).then_inc(silu_step, 1)
            dve.wait_ge(silu_step, 2)
            dve.tensor_tensor(silu_c[:, :], silu_r[:, :], cT_sb[:, :], ALU.mult).then_inc(silu_step, 1)
            dve.wait_ge(silu_step, 3)
            dve.wait_ge(zeroed, N_ZEROED)
            for p in range(2):
                dve.memset(Ks[p][SHIFT:SHIFT + NSHIFT, :, :], 1.0).then_inc(ones_ok, 1)
            for b in range(B):
                dve.tensor_scalar(silu_w[:, b, :], ones_w[:, :], silu_c[:, b:b + 1], None, ALU.mult).then_inc(silu_wide, 1)

            dve.wait_ge(mod_mm, 1)
            dve.tensor_copy(mod[:, :, :], bank_s[0][:, 0:6 * B].rearrange("p (j b) -> p j b", b=B)).then_inc(mod_ok, 1)
            dve.wait_ge(mod_ok, 1)
            for j in (1, 4):
                dve.tensor_scalar(mod[:, j, :], mod[:, j, :], 1.0, None, ALU.add).then_inc(mod_ok, 1)
            count = 3
            dve.wait_ge(mod_mm, 2)
            dve.tensor_copy(raw_a[:, :, :], bank_s[1][:, 0:B * C].rearrange("p (b c) -> p b c", b=B)).then_inc(mod_ok, 1)
            dve.wait_ge(mod_ok, 4)
            for raw, s2, mg, gate in ((raw_a[:, :, :], sgn[:, :, :], mag[:, :, :], ga_b[:, :, :]),
                                      (mod[:, 5, :], gsgn[:, :], gmag[:, :], gb_c[:, :])):
                base = 4 if gate.shape[-1] == C else 8
                dve.tensor_scalar(s2, raw, 0.0, 2.0, ALU.is_ge, ALU.mult).then_inc(mod_ok, 1)
                dve.scalar_tensor_tensor(out=mg, in0=raw, scalar=-1.0, in1=raw, op0=ALU.mult, op1=ALU.max).then_inc(mod_ok, 1)
                dve.wait_ge(mod_ok, base + 2)
                dve.tensor_scalar(mg, mg, 0.25, None, ALU.max).then_inc(mod_ok, 1)
                dve.wait_ge(mod_ok, base + 3)
                dve.scalar_tensor_tensor(out=gate, in0=s2, scalar=-1.0, in1=mg, op0=ALU.add, op1=ALU.mult).then_inc(mod_ok, 1)

            def normalise(b):
                dve.wait_ge(ln_rstd, b + 1)
                for t in range(b * KT, (b + 1) * KT):
                    dve.tensor_scalar(xn[:, t, :], x_sb[:, t, :], mv[:, t, 0:1], rstd[:, t:t + 1],
                                      ALU.subtract, ALU.mult).then_inc(ln_done, 1)

            def rope(n):
                half = slice((n % 2) * TB, (n % 2 + 1) * TB)
                for w in range(2):
                    k = 2 * n + w
                    wait(dve, rope_sum, k - 1)
                    dve.wait_ge(qk_mm, 2 * k + 1)
                    dve.scalar_tensor_tensor(out=rope_a[:, w, :], in0=bank_m[w][:, 0:TB], scalar=bqk_sb[:, 2 * w:2 * w + 1],
                                             in1=cos_sb[:, half], op0=ALU.add, op1=ALU.mult).then_inc(rope_half, 1)
                    dve.wait_ge(qk_mm, 2 * k + 2)
                    dve.scalar_tensor_tensor(out=rope_b[:, w, :], in0=bank_m[w][:, TB:2 * TB],
                                             scalar=bqk_sb[:, 2 * w + 1:2 * w + 2],
                                             in1=sin_sb[:, half], op0=ALU.add, op1=ALU.mult).then_inc(rope_half, 1)
                    dve.wait_ge(rope_half, 2 * k + 2)
                    wait(dve, part_hi, k - 1)
                    wait(dve, part_rest, k - 1)
                    dve.tensor_tensor(roped[:, w, :], rope_a[:, w, :], rope_b[:, w, :], ALU.add).then_inc(rope_sum, 1)

            def value_bias(n):
                dve.wait_ge(v_mm, n + 1)
                dve.tensor_tensor(v_all[:, n * BT:(n + 1) * BT, :], bank_x[:, :].rearrange("p (t c) -> p t c", t=BT),
                                  bv_sb[:, :].unsqueeze(1).broadcast_to([P, BT, C]), ALU.add).then_inc(v_ok, 1)

            normalise(0)
            dve.wait_ge(in_rope, 32)
            for n in range(NBLK):
                rope(n)
                if n == 0:
                    normalise(1)
                value_bias(n)

            dve.wait_ge(in_late, 16 * N_LATE)
            dve.wait_ge(pad_init, 2)
            rows = slice(0, 3 * E)
            dve.tensor_copy(b2_parts[rows, 0, :], b2_sb[rows, :]).then_inc(b2_step, 1)
            dve.wait_ge(b2_step, 1)
            dve.tensor_tensor(b2_r[rows, :], b2_sb[rows, :], b2_parts[rows, 0, :], ALU.subtract).then_inc(b2_step, 1)
            dve.wait_ge(b2_step, 2)
            dve.tensor_copy(b2_parts[rows, 1, :], b2_r[rows, :]).then_inc(b2_step, 1)
            dve.wait_ge(b2_step, 3)
            dve.tensor_tensor(b2_parts[rows, 2, :], b2_r[rows, :], b2_parts[rows, 1, :], ALU.subtract).then_inc(b2_step, 1)

            def maxima(m, q, r):
                dve.wait_ge(max_mm, m * MAXU + r + 1)
                wait(dve, shift_lo, (m - 2) * HG + r // BT + 1)
                dve.tensor_reduce(neg_max[q][:, r:r + 1], bank_m[r % 2][:, :], AX.X, ALU.max,
                                  negate=True).then_inc(max_ok, 1)
                if r % BT == BT - 1:
                    hh = r // BT
                    cols = slice(hh * BT, (hh + 1) * BT)
                    dve.wait_ge(max_ok, m * MAXU + r + 1)
                    wait(dve, shift_tr, (m - 2) * HG + hh + 1)
                    dve.tensor_copy(shift_parts[q][:, cols, 0], neg_max[q][:, cols]).then_inc(shift_hi, 1)
                    dve.wait_ge(shift_hi, m * HG + hh + 1)
                    dve.tensor_tensor(shift_parts[q][:, cols, 1], neg_max[q][:, cols], shift_parts[q][:, cols, 0],
                                      ALU.subtract).then_inc(shift_lo, 1)

            def divide(n, where):
                dve.wait_ge(o_tr, n + 1)
                wait(dve, attn_ok, n)
                o4 = bank_x[:, :].rearrange("p (t h w) -> p t h w", t=BT, h=HG)
                dve.reciprocal(rden[:, :].rearrange("p (t h) -> p t h", t=BT), o4[:, :, :, D]).then_inc(rden_ok, 1)
                dve.wait_ge(rden_ok, n + 1)
                dve.tensor_tensor(where, o4[:, :, :, 0:D],
                                  rden[:, :].rearrange("p (t h) -> p t h", t=BT).unsqueeze(3).broadcast_to([P, BT, HG, D]),
                                  ALU.mult).then_inc(attn_ok, 1)

            attn_g = attn[:, :, :].rearrange("p (n t) c -> p n t c", n=NBLK)

            def attn_at(pair, p):
                blk = pair >> 1
                g = (pair & 1) * 2 + p
                return attn_g[:, bass.ds(blk, 1), :, bass.ds(g * HG * D, HG * D)]\
                    .rearrange("p n t (h d) -> p (n t) h d", h=HG)

            def dve_step(pair, p, first, last):
                n = pair * 2 + p
                for r in range(MAXU):
                    if not last:
                        maxima(n + 1, 1 - p, r)
                    if r == 6 and not first:
                        divide(n - 1, attn_at(pair + p - 1, 1 - p))

            for r in range(MAXU):
                maxima(0, 0, r)
            dve_step(0, 0, True, False)
            dve_step(0, 1, False, False)
            with dve.Fori(1, NSTEP // 2 - 1) as pair:
                dve_step(pair, 0, False, False)
                dve_step(pair, 1, False, False)
            dve_step(NSTEP // 2 - 1, 0, False, False)
            dve_step(NSTEP // 2 - 1, 1, False, True)
            divide(NSTEP - 1, attn_at(NSTEP // 2 - 1, 1))

            def residual(n):
                r = slice(n * BT, (n + 1) * BT)
                dve.wait_ge(wo_mm, n + 1)
                dve.wait_ge(xbias_ok, B)
                dve.tensor_tensor(x1[:, r, :], bank_m[0][:, 0:TB].rearrange("p (t c) -> p t c", t=BT), x_sb[:, r, :],
                                  ALU.add).then_inc(x1_ok, 1)
                dve.wait_ge(x1_ok, n + 1)
                for t in range(n * BT, (n + 1) * BT):
                    dve.bn_stats(stats[:, t, :], x1[:, t, :]).then_inc(st2, 1)
                dve.wait_ge(st2, (n + 1) * BT)
                for t in range(n * BT, (n + 1) * BT):
                    dve.bn_aggr(mv[:, t, :], stats[:, t, :]).then_inc(mv2, 1)
                dve.wait_ge(mv2, (n + 1) * BT)
                dve.tensor_scalar(veps[:, r], mv[:, r, 1], EPS, None, ALU.add).then_inc(eps2, 1)
                dve.wait_ge(rstd2, n + 1)
                for t in range(n * BT, (n + 1) * BT):
                    dve.tensor_scalar(xn[:, t, :], x1[:, t, :], mv[:, t, 0:1], rstd[:, t:t + 1],
                                      ALU.subtract, ALU.mult).then_inc(xn2, 1)

            def route(n):
                dve.wait_ge(h2hi_ok, n + 1)
                cols = slice(n * TB, (n + 1) * TB)
                dve.tensor_tensor(h2_lo[:, cols], h2f[:, :], h2_hi[:, cols].bitcast(F32), ALU.subtract).then_inc(h2lo_ok, 1)
                dve.wait_ge(route_mm, n + 1)
                wait(dve, rexp_ok, n * BT)
                dve.tensor_tensor(logit[:, :, :], bank_m[1][:, 0:BT * E].rearrange("p (t e) -> p t e", t=BT),
                                  rb_sb[:, 0, :].unsqueeze(1).broadcast_to([P, BT, E]), ALU.add).then_inc(logit_ok, 1)
                dve.wait_ge(logit_ok, n + 1)
                dve.tensor_reduce(neg_lmax[:, :], logit[:, :, :], AX.X, ALU.max, negate=True).then_inc(lmax_ok, 1)
                base = n * N_TOP
                dve.wait_ge(rexp_ok, (n + 1) * BT)
                for t in range(BT):
                    dve.max(top8[:, t, :], ext[:, t, :]).then_inc(top_ok, 1)
                dve.wait_ge(top_ok, base + BT)
                dve.memset(top8[:, :, TOPK:8], -1.0).then_inc(top_ok, 1)
                dve.wait_ge(top_ok, base + BT + 1)
                for t in range(BT):
                    dve.match_replace(marked[:, t, :], top8[:, t, :], ext[:, t, :], -2.0).then_inc(top_ok, 1)
                dve.wait_ge(top_ok, base + 2 * BT + 1)
                dve.scalar_tensor_tensor(out=chosen[:, :, :], in0=marked[:, :, 0:E], scalar=-2.0, in1=ext[:, :, 0:E],
                                         op0=ALU.is_equal, op1=ALU.mult).then_inc(top_ok, 1)
                dve.wait_ge(top_ok, base + 2 * BT + 2)
                dve.tensor_reduce(csum[:, :], chosen[:, :, :], AX.X, ALU.add).then_inc(top_ok, 1)
                dve.wait_ge(top_ok, base + 2 * BT + 3)
                dve.reciprocal(crec[:, :], csum[:, :]).then_inc(top_ok, 1)
                dve.wait_ge(top_ok, base + 2 * BT + 4)
                dve.tensor_tensor(comb[:, :, :], chosen[:, :, :], crec[:, :].unsqueeze(2).broadcast_to([P, BT, E]),
                                  ALU.mult).then_inc(comb_ok, 1)
                dve.wait_ge(comb_ok, n + 1)
                wait(dve, comb_tr, n)
                dve.tensor_copy(comb_parts[:, :, 0, :], comb[:, :, :]).then_inc(top_ok, 1)
                dve.wait_ge(top_ok, base + 2 * BT + 5)
                dve.tensor_tensor(comb_r[:, :, :], comb[:, :, :], comb_parts[:, :, 0, :], ALU.subtract).then_inc(top_ok, 1)
                dve.wait_ge(top_ok, base + 2 * BT + 6)
                dve.tensor_copy(comb_parts[:, :, 1, :], comb_r[:, :, :]).then_inc(top_ok, 1)
                dve.wait_ge(top_ok, base + 2 * BT + 7)
                dve.tensor_tensor(comb_parts[:, :, 2, :], comb_r[:, :, :], comb_parts[:, :, 1, :], ALU.subtract).then_inc(top_ok, 1)

            for n in range(NBLK):
                residual(n)
                route(n)

            def expert_step(s, k):
                q = k % 2
                for c in range(ICH):
                    dve.wait_ge(gelu_ok, s * ICH + c + 1)
                    if c == 0:
                        dve.wait_ge(cb_mm, s + 1)
                    wait(dve, glo_ok, (s - 2) * ICH + c + 1)
                    dve.tensor_tensor(gc_sb[:, q, c, :], g_sb[:, q, c, :], bank_c[q], ALU.mult).then_inc(gc_ok, 1)
                for c in range(ICH):
                    dve.wait_ge(ghi_ok, s * ICH + c + 1)
                    wait(dve, y_mm, s - 1)
                    dve.tensor_tensor(g_lo[:, q, c, :], gc_sb[:, q, c, :], g_hi[:, q, c, :].bitcast(F32),
                                      ALU.subtract).then_inc(glo_ok, 1)

            for k in range(2 * NBLK):
                expert_step(k, k)
            with dve.Fori(1, E // 2) as i:
                for k in range(2 * NBLK):
                    expert_step(i * 2 * NBLK + k, k)

            for n in range(NBLK):
                dve.wait_ge(y_tr, n + 1)
                r = slice(n * BT, (n + 1) * BT)
                dve.tensor_tensor(x1[:, r, :], bank_r[n % 2].rearrange("p (t c) -> p t c", t=BT), x1[:, r, :],
                                  ALU.add).then_inc(out_ok, 1)

        @block.tensor
        def _(pe):
            pe.wait_ge(in_consts, 16 * N_CONST)
            pe.wait_ge(silu_step, 3)
            for j in range(6):
                mm = pe.matmul(bank_s[0][:, j * B:(j + 1) * B], wmod_sb[:, j, :], silu_c[:, :], start=True, stop=True)
            mm.then_inc(mod_mm, 1)
            pe.wait_ge(silu_wide, B)
            for b in range(B):
                mm = pe.matmul(bank_s[1][:, b * C:(b + 1) * C], silu_w[:, b, :], wmod_sb[:, 2, :], start=True, stop=True)
            mm.then_inc(mod_mm, 1)

            def transpose_x(n):
                pe.wait_ge(ln_done, (n + 1) * BT)
                wait(pe, hT_ok, n)
                for t in range(BT):
                    mm = pe.transpose(bank_o[:, t * P:(t + 1) * P], xn[:, n * BT + t, :], id_f[:, :])
                mm.then_inc(xT_mm, 1)

            def project(n):
                cols = slice(n * TB, (n + 1) * TB)
                pe.wait_ge(hT_ok, n + 1)
                for w in range(2):
                    for j in range(2):
                        wait(pe, rope_half, 4 * (n - 1) + 2 * w + j + 1)
                        pe.matmul(bank_m[w][:, j * TB:(j + 1) * TB], wqk_sb[:, 2 * w + j, :], hT[:, cols],
                                  start=True, stop=True).then_inc(qk_mm, 1)
                wait(pe, v_ok, n)
                for t in range(BT):
                    tok = n * TB + t * P
                    mm = pe.matmul(bank_x[:, t * C:(t + 1) * C], hT[:, tok:tok + P], wv_sb[:, :], start=True, stop=True)
                mm.then_inc(v_mm, 1)

            transpose_x(0)
            for n in range(NBLK):
                if n + 1 < NBLK:
                    transpose_x(n + 1)
                project(n)

            def max_unit(m, q, r):
                hh, t = r // BT, r % BT
                wait(pe, max_ok, m * MAXU + r - 1)
                for half in range(2):
                    mm = pe.matmul(bank_m[r % 2][:, half * TB:(half + 1) * TB], Qs[q][:, hh, t * P:(t + 1) * P],
                                   Ks[q][:, hh, half * TB:(half + 1) * TB], start=True, stop=True)
                mm.then_inc(max_mm, 1)

            def turn_shift(m, q, hh):
                pe.wait_ge(shift_lo, m * HG + hh + 1)
                wait(pe, shift_ok, m * HG + hh)
                for t in range(BT):
                    mm = pe.transpose(shift_psum[:, t * P:(t + 1) * P], shift_parts[q][:, hh * BT + t, :], id_b[:, :])
                mm.then_inc(shift_tr, 1)

            def scores(n, p, kt, hh):
                u = kt * HG + hh
                wait(pe, exp_ok, n * UNITS + u - 1)
                if kt == 0:
                    pe.wait_ge(shift_ok, n * HG + hh + 1)
                pe.matmul(bank_s[u % 2][:, :], Ks[p][:, hh, kt * P:(kt + 1) * P], Qs[p][:, hh, :],
                          start=True, stop=True).then_inc(score_mm, 1)

            def products(n, p, kt):
                pe.wait_ge(exp_ok, n * UNITS + (kt + 1) * HG)
                if kt == 0:
                    pe.wait_ge(v_staged, n + 1)
                    wait(pe, oT_ok, n)
                for hh in range(HG):
                    mm = pe.matmul(bank_o[hh * VW:(hh + 1) * VW, :], Vs[p][:, kt, hh, :],
                                   prob[:, (kt * HG + hh) % RING, :], start=(kt == 0), stop=(kt == KT - 1))
                mm.then_inc(pv_mm, 1)

            def turn_sums(n):
                pe.wait_ge(oT_ok, n + 1)
                wait(pe, attn_ok, n)
                for t in range(BT):
                    mm = pe.transpose(bank_x[:, t * P:(t + 1) * P], oT[:, t * P:(t + 1) * P], id_f[:, :])
                mm.then_inc(o_tr, 1)

            def pe_step(n, p, first, last):
                m, q = n + 1, 1 - p
                for kt in range(KT):
                    scores(n, p, kt, 0)
                    scores(n, p, kt, 1)
                    units = [] if last else list(range(MAX_FROM[kt], MAX_FROM[kt + 1]))
                    if kt == 0 and not last:
                        pe.wait_ge(staged[q], staged_count(m, q))
                        max_unit(m, q, units.pop(0))
                    if kt == 0 and not first:
                        turn_shift(n, p, HG - 1)
                    if kt > 0:
                        products(n, p, kt - 1)
                    elif not first:
                        products(n - 1, q, KT - 1)
                    scores(n, p, kt, 2)
                    scores(n, p, kt, 3)
                    for r in units:
                        max_unit(m, q, r)
                    if kt == 2 and not first:
                        pe.wait_ge(shift_ok, n * HG + HG)
                        turn_sums(n - 1)
                    if kt in (4, 5, 6) and not last:
                        if kt == 4:
                            wait(pe, attn_ok, n)
                        turn_shift(m, q, kt - 4)

            def staged_count(m, q):
                return 48 * ((m - q) // 2 + 1) if isinstance(m, int) else ((m - q) >> 1) * 48 + 48

            pe.wait_ge(rope_half, 4 * NBLK)
            pe.wait_ge(v_ok, NBLK)
            pe.wait_ge(hT_ok, NBLK)
            pe.wait_ge(mod_ok, N_MOD)
            pe.wait_ge(staged[0], 48)
            for r in range(MAXU):
                max_unit(0, 0, r)
                if r % BT == BT - 1 and r > BT:
                    turn_shift(0, 0, r // BT - 1)
            turn_shift(0, 0, HG - 1)
            pe_step(0, 0, True, False)
            pe_step(1, 1, False, False)
            with pe.Fori(1, NSTEP // 2 - 1) as i:
                pe_step(i * 2, 0, False, False)
                pe_step(i * 2 + 1, 1, False, False)
            pe_step(NSTEP - 2, 0, False, False)
            pe_step(NSTEP - 1, 1, False, True)
            products(NSTEP - 1, 1, KT - 1)
            turn_sums(NSTEP - 1)

            pe.wait_ge(gate_ok, 2 * B)
            for n in range(NBLK):
                if n == 0:
                    pe.wait_ge(attn_ok, NSTEP)
                for t in range(BT):
                    mm = pe.transpose(bank_o[:, t * P:(t + 1) * P], attn[:, n * BT + t, :], id_f[:, :])
                mm.then_inc(a_tr, 1)
                pe.wait_ge(aT_ok, n + 1)
                for t in range(BT):
                    mm = pe.matmul(bank_m[0][:, t * C:(t + 1) * C], attnT[:, t * P:(t + 1) * P], wo_g[:, n // 2, :],
                                   start=True, stop=True)
                mm.then_inc(wo_mm, 1)
                pe.wait_ge(xn2, (n + 1) * BT)
                for t in range(BT):
                    mm = pe.transpose(bank_m[0][:, TB + t * P:TB + (t + 1) * P], xn[:, n * BT + t, :], id_f[:, :])
                mm.then_inc(x2_tr, 1)
                pe.wait_ge(h2_ok, n + 1)
                for t in range(BT):
                    mm = pe.matmul(bank_m[1][:, t * E:(t + 1) * E], h2f[:, t * P:(t + 1) * P], rw_sb[:, :],
                                   start=True, stop=True)
                mm.then_inc(route_mm, 1)
                pe.wait_ge(top_ok, (n + 1) * N_TOP)
                for t in range(BT):
                    mm = pe.transpose(comb_psum[:, t * P:(t + 1) * P],
                                      comb_parts[:, t, :, :].rearrange("p a e -> p (a e)"), id_b[:, :])
                mm.then_inc(comb_tr, 1)
                pe.wait_ge(combT_ok, n + 1)

            pe.wait_ge(b2_step, 4)
            for n in range(NBLK):
                for i in range(3):
                    pe.matmul(bank_y[n], b2_parts[:, i, :], combT[:, n * TB:(n + 1) * TB], start=(i == 0), stop=False,
                              skip_group_check=True)

            def expert_hidden(e, s, k):
                n, p, q = k % NBLK, k // NBLK, k % 2
                cols = slice(n * TB, (n + 1) * TB)
                if n == 0:
                    pe.wait_ge(w_lo_ok, e + 1)
                wait(pe, gc_ok, (s - 1) * ICH)
                pe.matmul(bank_c[q], select_sb[:, bass.ds(e, 1), :].rearrange("k e m -> k (e m)"), combT[:, cols],
                          start=True, stop=True).then_inc(cb_mm, 1)
                for c in range(ICH):
                    part = slice(c * P, (c + 1) * P)
                    wait(pe, gelu_ok, (s - 1) * ICH + c + 1)
                    pe.matmul(bank_h[c], w_hi[p][:, 0, part], h2_hi[:, cols], start=True, stop=False)
                    pe.matmul(bank_h[c], w_hi[p][:, 0, part], h2_lo[:, cols], start=False, stop=False)
                    pe.matmul(bank_h[c], w_lo[p][:, 0, part], h2_hi[:, cols], start=False, stop=True).then_inc(h_mm, 1)

            def expert_sum(s, k):
                n, p, q = k % NBLK, k // NBLK, k % 2
                for c in range(ICH):
                    part = slice(c * C, (c + 1) * C)
                    pe.wait_ge(ghi_ok, s * ICH + c + 1)
                    pe.matmul(bank_y[n], w_hi[p][:, 1, part], g_hi[:, q, c, :], start=False, stop=False, skip_group_check=True)
                    pe.matmul(bank_y[n], w_lo[p][:, 1, part], g_hi[:, q, c, :], start=False, stop=False, skip_group_check=True)
                    pe.wait_ge(glo_ok, s * ICH + c + 1)
                    mm = pe.matmul(bank_y[n], w_hi[p][:, 1, part], g_lo[:, q, c, :], start=False, stop=True, skip_group_check=True)
                mm.then_inc(y_mm, 1)

            LAST = 2 * NBLK - 1
            pe.wait_ge(h2lo_ok, NBLK)
            expert_hidden(0, 0, 0)
            for k in range(LAST):
                expert_hidden((k + 1) // NBLK, k + 1, k + 1)
                expert_sum(k, k)
            with pe.Fori(1, E // 2) as i:
                for k in range(-1, LAST):
                    expert_hidden(i * 2 + (k + 1) // NBLK, i * 2 * NBLK + k + 1, k + 1)
                    expert_sum(i * 2 * NBLK + k, k % (2 * NBLK))
            expert_sum(E * NBLK - 1, LAST)

            for n in range(NBLK):
                pe.wait_ge(yT_ok, n + 1)
                wait(pe, out_ok, n - 1)
                for t in range(BT):
                    mm = pe.transpose(bank_r[n % 2][:, t * P:(t + 1) * P], yT[:, n % 2, t * P:(t + 1) * P], id_f[:, :])
                mm.then_inc(y_tr, 1)


def kernel(L0_attn_x, L0_attn_Wq, L0_attn_bq, L0_attn_Wk, L0_attn_bk, L0_attn_Wv, L0_attn_bv, L0_attn_Wo, L0_attn_bo,
           L0_ffn_router_w, L0_ffn_router_b, L0_ffn_w1, L0_ffn_b1, L0_ffn_w2, L0_ffn_b2, L0_c, L0_wmod):
    import numpy as np
    import concourse.bacc as bacc
    from concourse.bass_utils import run_bass_kernel_spmd

    f32 = np.float32
    swap = np.arange(H * D).reshape(H, 2, D // 2)[:, ::-1].reshape(-1)
    theta = f32(10000.0) ** (-np.arange(D // 2, dtype=f32) / f32(D // 2))
    angle = np.arange(T, dtype=f32)[:, None] * theta[None, :]
    cos = np.tile(np.cos(angle).T, (2 * H, 1)).astype(f32)
    sin = np.tile(np.concatenate([-np.sin(angle).T, np.sin(angle).T]), (H, 1)).astype(f32)
    row = np.arange(P)
    select = ((row[:, None] % E == np.arange(E)[None, :]) & (row[:, None] < 3 * E))
    select = np.repeat(select[:, :, None], P, axis=2).reshape(P, E * P)
    bf16 = mybir.dt.np(BF16)
    wq, wk = np.asarray(L0_attn_Wq), np.asarray(L0_attn_Wk)
    bq, bk = np.asarray(L0_attn_bq), np.asarray(L0_attn_bk)
    arrays = {
        "x": np.asarray(L0_attn_x),
        "wqkT": np.stack([wq.T, wq[swap].T, wk.T, wk[swap].T]),
        "bqk": np.stack([bq, bq[swap], bk, bk[swap]], axis=1),
        "wvT": np.asarray(L0_attn_Wv).T,
        "bv": np.asarray(L0_attn_bv),
        "woT": np.asarray(L0_attn_Wo).T,
        "bo": np.asarray(L0_attn_bo),
        "router_w": np.asarray(L0_ffn_router_w),
        "router_b": np.asarray(L0_ffn_router_b),
        "w1": np.asarray(L0_ffn_w1),
        "b1T": np.asarray(L0_ffn_b1).reshape(E * ICH, P).T,
        "w2": np.asarray(L0_ffn_w2),
        "b2": np.asarray(L0_ffn_b2),
        "cT": np.asarray(L0_c).T,
        "wmod": np.asarray(L0_wmod),
        "cos": cos,
        "sin": sin,
        "ident": np.eye(P, dtype=f32),
        "identb": np.eye(P).astype(bf16),
        "select": select.astype(bf16),
    }
    nc = bacc.Bacc("TRN2", target_bir_lowering=False, num_devices=1)
    feeds, args = {}, []
    for name, a in arrays.items():
        a = np.ascontiguousarray(a)
        feeds[f"in_{name}"] = a
        args.append(nc.dram_tensor(f"in_{name}", a.shape, mybir.dt.from_np(a.dtype), kind="ExternalInput").ap())
    args.append(nc.dram_tensor("out_dram", (B, T, C), F32, kind="ExternalOutput").ap())
    block_program(nc, *args)
    r = run_bass_kernel_spmd(nc, [feeds], core_ids=[0])
    return r.results[0]["out_dram"]
```

```python
from contextlib import ExitStack

import concourse.bass as bass
from concourse import mybir

F32 = mybir.dt.float32
F32R = mybir.dt.float32r
BF16 = mybir.dt.bfloat16
ALU = mybir.AluOpType
ACT = mybir.ActivationFunctionType
AX = mybir.AxisListType

P = 128
B, T, C = 2, 1024, 128
H, D = 16, 8
E, I = 16, 256
TOPK = 4
TB = 512
NBLK = B * T // TB
NT = B * T // P
BT = TB // P
HG = 4
NG = H // HG
KT = T // P
NSTEP = NBLK * NG
VW = 32
TERMS = 6
ROWS = D * TERMS
SHIFT = 64
NSHIFT = 2
UNITS = KT * HG
MAXU = HG * BT
RING = 8
NBUF = 3
Q_PART = (0, 0, 0, 1, 1, 2)
K_PART = (0, 1, 2, 0, 1, 0)
ICH = I // P
EPS = 1e-5
LOOPS = (NSTEP - 4) // NBUF
MAX_PLAN = (2, 2, 2, 2, 2, 2, 2, 2)
SHIFT_AT = (3, 5, 6)
MAX_FROM = tuple(sum(MAX_PLAN[:k]) for k in range(KT + 1))


def block_program(nc: bass.Bass, x, wqkT, bqk, wvT, bv, woT, bo, router_w, router_b, w1, b1T, w2, b2,
                  cT, wmod, cos, sin, ident, identb, select, out):
    ctx = ExitStack()
    with ctx:
        def sb(name, shape, dt=F32):
            return ctx.enter_context(nc.sbuf_tensor(name, shape, dt))

        passing = ExitStack()

        projecting = ExitStack()

        def sbp(name, shape, dt=F32):
            return projecting.enter_context(nc.sbuf_tensor(name, shape, dt))

        def sba(name, shape, dt=F32):
            return passing.enter_context(nc.sbuf_tensor(name, shape, dt))

        def psum(name, shape, dt=F32):
            return ctx.enter_context(nc.psum_tensor(name, shape, dt))

        def sem(name):
            return ctx.enter_context(nc.semaphore(name))

        q_rows = nc.dram_tensor("q_rows", [NBLK, H * D, TERMS, TB], BF16, kind="Internal").ap()
        k_rows = nc.dram_tensor("k_rows", [B, H * D, TERMS, T], BF16, kind="Internal").ap()

        x_sb = sb("x_sb", [P, NT, C])
        xn = sb("xn", [P, NT, C])
        id_f = sb("id_f", [P, P])
        id_b = sb("id_b", [P, P], BF16)
        wqk_sb = sb("wqk_sb", [P, 4, C])
        bqk_sb = sb("bqk_sb", [P, 4])
        wv_sb = sb("wv_sb", [P, C])
        bv_sb = sb("bv_sb", [P, C])
        wo_sb = sb("wo_sb", [P, C])
        wo_g = sb("wo_g", [P, B, C])
        bo_sb = sb("bo_sb", [P, C])
        bo_g = sb("bo_g", [P, B, C])
        cT_sb = sb("cT_sb", [P, B])
        silu_e = sb("silu_e", [P, B])
        silu_d = sb("silu_d", [P, B])
        silu_r = sb("silu_r", [P, B])
        silu_c = sb("silu_c", [P, B])
        silu_w = sb("silu_w", [P, B, P])
        ones_w = sb("ones_w", [P, P])
        wmod_sb = sb("wmod_sb", [P, 6, C])
        mod = sb("mod", [P, 6, B])
        raw_a = sb("raw_a", [P, B, C])
        sgn = sb("sgn", [P, B, C])
        mag = sb("mag", [P, B, C])
        ga_b = sb("ga_b", [P, B, C])
        gsgn = sb("gsgn", [P, B])
        gmag = sb("gmag", [P, B])
        gb_c = sb("gb_c", [P, B])
        stats = sb("stats", [P, NT, 6])
        mv = sb("mv", [P, NT, 2])
        veps = sb("veps", [P, NT])
        neg_half = sb("neg_half", [P, NT])
        rstd = sb("rstd", [P, NT])
        neg_max = [sb(f"neg_max{i}", [P, MAXU]) for i in range(NBUF)]
        shift_parts = [sb(f"shift_parts{i}", [P, MAXU, NSHIFT], BF16) for i in range(NBUF)]
        rden = sb("rden", [P, BT * HG])
        attn = sb("attn", [P, NT, C])
        rw_sb = sb("rw_sb", [P, E])
        rb_sb = sb("rb_sb", [P, BT, E])
        logit = sb("logit", [P, BT, E])
        neg_lmax = sb("neg_lmax", [P, BT])
        ext = sb("ext", [P, BT, E + TOPK])
        top8 = sb("top8", [P, BT, 8])
        marked = sb("marked", [P, BT, E + TOPK])
        chosen = sb("chosen", [P, BT, E])
        csum = sb("csum", [P, BT])
        crec = sb("crec", [P, BT])
        comb = sb("comb", [P, BT, E])
        comb_r = sb("comb_r", [P, BT, E])
        comb_parts = sb("comb_parts", [P, BT, 3, E], BF16)
        combT = sb("combT", [P, B * T], BF16)
        select_sb = sb("select_sb", [P, E, P], BF16)
        b2_sb = sb("b2_sb", [3 * E, C])
        b2_r = sb("b2_r", [3 * E, C])
        b2_parts = sb("b2_parts", [P, 3, C], BF16)
        b1_sb = sb("b1_sb", [P, E * ICH])
        hT = sbp("hT", [P, B * T])
        cos_sb = sbp("cos_sb", [P, T])
        sin_sb = sbp("sin_sb", [P, T])
        rope_a = sbp("rope_a", [P, 2, TB])
        rope_b = sbp("rope_b", [P, 2, TB])
        roped = sbp("roped", [P, 2, TB])
        rest = sbp("rest", [P, 2, TB])
        projecting.close()
        x1 = sb("x1", [P, NT, C])
        attnT = sb("attnT", [P, NBLK, TB])
        h2f = sb("h2f", [P, NBLK, TB])
        h2_hi = sb("h2_hi", [P, B * T], F32R)
        h2_lo = sb("h2_lo", [P, B * T], F32R)
        q_part = sba("q_part", [P, 3, NBLK, TB], BF16)
        k_part = sba("k_part", [P, 3, NBLK, TB], BF16)
        v_all = sba("v_all", [P, NT, H * D])
        Qs = [sba(f"Qs{i}", [P, HG, TB], BF16) for i in range(NBUF)]
        Ks = [sba(f"Ks{i}", [P, HG, T], BF16) for i in range(NBUF)]
        Vs = [sba(f"Vs{i}", [P, KT, HG, VW]) for i in range(NBUF)]
        zrow = sba("zrow", [NSHIFT, HG * TB], BF16)
        prob = sba("prob", [P, RING, TB])
        oT = sba("oT", [P, TB])
        passing.close()
        bias = [sb(f"bias{i}", [P, ICH]) for i in range(2)]
        w_st = [sb(f"w_st{i}", [P, 2, I]) for i in range(2)]
        w_hi = [sb(f"w_hi{i}", [P, 2, I], F32R) for i in range(2)]
        w_lo = [sb(f"w_lo{i}", [P, 2, I], F32R) for i in range(2)]
        g_sb = sb("g_sb", [P, 2, ICH, TB])
        gc_sb = sb("gc_sb", [P, 2, ICH, TB])
        g_hi = sb("g_hi", [P, 2, ICH, TB], F32R)
        g_lo = sb("g_lo", [P, 2, ICH, TB], F32R)
        yT = sb("yT", [P, 2, TB])

        bank_s = [psum(f"bank_s{i}", [P, TB]) for i in range(2)]
        bank_m = [psum(f"bank_m{i}", [P, 2 * TB]) for i in range(2)]
        bank_o = psum("bank_o", [P, TB])
        bank_x = psum("bank_x", [P, TB])

        shift_psum = bank_x[:, :].bitcast(BF16)[SHIFT:SHIFT + NSHIFT, 0:TB]
        comb_psum = bank_m[1][:, TB:2 * TB].bitcast(BF16)[0:3 * E, 0:TB]
        bank_y = [bank_s[0][:, :], bank_s[1][:, :], bank_o[:, :], bank_x[:, :]]
        bank_h = [bank_m[0][:, 0:TB], bank_m[0][:, TB:2 * TB]]
        bank_c = [bank_m[1][:, 0:TB], bank_m[1][:, TB:2 * TB]]
        bank_r = bank_h

        in_consts = sem("in_consts")
        in_x = [sem(f"in_x{b}") for b in range(B)]
        in_rope = sem("in_rope")
        in_late = sem("in_late")
        zeroed = sem("zeroed")
        ones_ok = sem("ones_ok")
        silu_exp = sem("silu_exp")
        silu_step = sem("silu_step")
        silu_wide = sem("silu_wide")
        mod_mm = sem("mod_mm")
        mod_ok = sem("mod_ok")
        gate_ok = sem("gate_ok")
        ln_stat = sem("ln_stat")
        ln_mv = sem("ln_mv")
        ln_eps = sem("ln_eps")
        ln_rstd = sem("ln_rstd")
        ln_done = sem("ln_done")
        xT_mm = sem("xT_mm")
        hT_ok = sem("hT_ok")
        qk_mm = sem("qk_mm")
        rope_half = sem("rope_half")
        rope_sum = sem("rope_sum")
        part_hi = sem("part_hi")
        part_rest = sem("part_rest")
        part_mid = sem("part_mid")
        part_lo = sem("part_lo")
        v_mm = sem("v_mm")
        v_ok = sem("v_ok")
        rows_out = sem("rows_out")
        staged = [sem(f"staged{i}") for i in range(NBUF)]
        v_staged = sem("v_staged")
        max_mm = sem("max_mm")
        max_ok = sem("max_ok")
        shift_hi = sem("shift_hi")
        shift_lo = sem("shift_lo")
        shift_tr = sem("shift_tr")
        shift_ok = sem("shift_ok")
        score_mm = sem("score_mm")
        exp_ok = sem("exp_ok")
        pv_mm = sem("pv_mm")
        oT_ok = sem("oT_ok")
        o_tr = sem("o_tr")
        rden_ok = sem("rden_ok")
        attn_ok = sem("attn_ok")
        a_tr = sem("a_tr")
        aT_ok = sem("aT_ok")
        wo_mm = sem("wo_mm")
        x1_ok = sem("x1_ok")
        xbias_ok = sem("xbias_ok")
        st2 = sem("st2")
        mv2 = sem("mv2")
        eps2 = sem("eps2")
        rstd2 = sem("rstd2")
        xn2 = sem("xn2")
        x2_tr = sem("x2_tr")
        h2_ok = sem("h2_ok")
        h2hi_ok = sem("h2hi_ok")
        h2lo_ok = sem("h2lo_ok")
        route_mm = sem("route_mm")
        logit_ok = sem("logit_ok")
        lmax_ok = sem("lmax_ok")
        rexp_ok = sem("rexp_ok")
        ext_init = sem("ext_init")
        pad_init = sem("pad_init")
        top_ok = sem("top_ok")
        comb_ok = sem("comb_ok")
        comb_tr = sem("comb_tr")
        combT_ok = sem("combT_ok")
        b2_step = sem("b2_step")
        w_in = [sem(f"w_in{i}") for i in range(2)]
        bias_ok = sem("bias_ok")
        w_hi_ok = sem("w_hi_ok")
        w_lo_ok = sem("w_lo_ok")
        cb_mm = sem("cb_mm")
        h_mm = sem("h_mm")
        gelu_ok = sem("gelu_ok")
        gc_ok = sem("gc_ok")
        ghi_ok = sem("ghi_ok")
        glo_ok = sem("glo_ok")
        y_mm = sem("y_mm")
        yT_ok = sem("yT_ok")
        y_tr = sem("y_tr")
        out_ok = sem("out_ok")
        stored = sem("stored")

        N_MOD = 12
        N_TOP = 2 * BT + 8
        N_CONST, N_LATE, N_ZEROED = 12, 5, 2 * NBUF + 3 + NBUF

        def wait(eng, s, value):
            if isinstance(value, int) and value <= 0:
                return
            eng.wait_ge(s, value)

        def by_steps(eng, first, count, body):
            lone = range(first, first + 2) if first == 0 else range(first + count - 2, first + count)
            rest = [m for m in range(first, first + count) if m not in lone]
            if first == 0:
                for m in lone:
                    body(m, m % NBUF)
            with eng.Fori(0, len(rest) // NBUF) as i:
                for k in range(NBUF):
                    body(i * NBUF + (rest[0] + k), (rest[0] + k) % NBUF)
            if first != 0:
                for m in lone:
                    body(m, m % NBUF)

        def stage(sp, b, m, p):
            wait(sp, score_mm, (m - NBUF + 1) * UNITS)
            heads = bass.ds((m & (NG - 1)) * (HG * D), HG * D)
            sp.dma_start(Qs[p][0:ROWS, :, :], q_rows.rearrange("n r e t -> (n r) e t")[bass.ds(m * (HG * D), HG * D), :, :]
                         .rearrange("(h d) e t -> (d e) h t", h=HG)).then_inc(staged[p], 16)
            sp.dma_start(Ks[p][0:ROWS, :, :], k_rows[b, heads, :, :]
                         .rearrange("(h d) e t -> (d e) h t", h=HG)).then_inc(staged[p], 16)
            sp.dma_start(Qs[p][SHIFT:SHIFT + NSHIFT, :, :],
                         zrow[:, :].rearrange("p (h t) -> p h t", h=HG)).then_inc(staged[p], 16)

        def load_weights(sp, e, p):
            wait(sp, w_lo_ok, e - 1)
            sp.dma_start(w_st[p][:, 0, :],
                         w1[bass.ds(e, 1), :, :].rearrange("e c i -> (e c) i")).then_inc(w_in[p], 16)
            sp.dma_start(w_st[p][:, 1, :].rearrange("p (h c) -> p h c", h=ICH),
                         w2[bass.ds(e, 1), :, :].rearrange("e (h p) c -> p (e h) c", h=ICH)).then_inc(w_in[p], 16)

        def cut_weights(pool, e, p, nth):
            pool.wait_ge(w_in[p], nth * 32)
            wait(pool, y_mm, (e - 1) * NBLK)
            pool.tensor_tensor(w_hi[p][:, :, :], w_st[p][:, :, :],
                               ones_w[:, 0:1].unsqueeze(2).broadcast_to([P, 2, I]), ALU.mult).then_inc(w_hi_ok, 1)
            pool.tensor_tensor(bias[p][:, :], b1_sb[:, bass.ds(e * ICH, ICH)], ones_w[:, 0:ICH],
                               ALU.mult).then_inc(bias_ok, 1)
            pool.wait_ge(w_hi_ok, e + 1)
            pool.tensor_tensor(w_lo[p][:, :, :], w_st[p][:, :, :], w_hi[p][:, :, :].bitcast(F32),
                               ALU.subtract).then_inc(w_lo_ok, 1)

        block = ctx.enter_context(nc.Block())

        @block.sync
        def _(sp):
            x_t = x.rearrange("b (n p) c -> p (b n) c", p=P)
            for b in range(B):
                sp.dma_start(x_sb[:, b * KT:(b + 1) * KT, :], x_t[:, b * KT:(b + 1) * KT, :]).then_inc(in_x[b], 16)
            sp.dma_start(cT_sb[:, :], cT).then_inc(in_consts, 16)
            sp.dma_start(wmod_sb[:, :, :], wmod.rearrange("k (j c) -> k j c", j=6)).then_inc(in_consts, 16)
            sp.dma_start(id_f[:, :], ident).then_inc(in_consts, 16)
            sp.dma_start(id_b[:, :], identb).then_inc(in_consts, 16)
            sp.dma_start(wqk_sb[:, :, :], wqkT.rearrange("j c o -> c j o")).then_inc(in_consts, 16)
            sp.dma_start(bqk_sb[:, :], bqk).then_inc(in_consts, 16)
            sp.dma_start(wv_sb[:, :], wvT).then_inc(in_consts, 16)
            sp.dma_start(wo_sb[:, :], woT).then_inc(in_consts, 16)
            sp.dma_start(bv_sb[:, :], bv.partition_broadcast(P)).then_inc(in_consts, 16)
            sp.dma_start(bo_sb[:, :], bo.partition_broadcast(P)).then_inc(in_consts, 16)
            sp.dma_start(rw_sb[:, :], router_w).then_inc(in_consts, 16)
            sp.dma_start(rb_sb[:, 0, :], router_b.partition_broadcast(P)).then_inc(in_consts, 16)
            sp.dma_start(cos_sb[:, :], cos).then_inc(in_rope, 16)
            sp.dma_start(sin_sb[:, :], sin).then_inc(in_rope, 16)

            sp.dma_start(b1_sb[:, :], b1T).then_inc(in_late, 16)
            for i in range(3):
                sp.dma_start(b2_sb[i * E:(i + 1) * E, :], b2).then_inc(in_late, 16)
            sp.dma_start(select_sb[:, :, :], select.rearrange("k (e m) -> k e m", e=E)).then_inc(in_late, 16)

            for b in range(B):
                sp.wait_ge(part_hi, 4 * (b + 1))
                sp.wait_ge(part_mid, 4 * (b + 1))
                sp.wait_ge(part_lo, 4 * (b + 1))
                for t in range(TERMS):
                    sp.dma_start(k_rows[b, :, t, :].rearrange("p (j t) -> p j t", j=2),
                                 k_part[:, K_PART[t], 2 * b:2 * b + 2, :]).then_inc(rows_out, 16)
                    sp.dma_start(q_rows[2 * b:2 * b + 2, :, t, :].rearrange("j p t -> p j t"),
                                 q_part[:, Q_PART[t], 2 * b:2 * b + 2, :]).then_inc(rows_out, 16)
                sp.wait_ge(rows_out, 16 * 2 * TERMS * (b + 1))
                if b == 0:
                    sp.wait_ge(zeroed, N_ZEROED)
                    sp.wait_ge(ones_ok, NBUF)
                by_steps(sp, b * 2 * NG, 2 * NG, lambda m, p, b=b: stage(sp, b, m, p))
            load_weights(sp, 0, 0)
            load_weights(sp, 1, 1)
            with sp.Fori(1, E // 2) as pair:
                for p in range(2):
                    load_weights(sp, pair * 2 + p, p)

            o_t = out.rearrange("b (n p) c -> p (b n) c", p=P)
            for n in range(NBLK):
                sp.wait_ge(out_ok, n + 1)
                sp.dma_start(o_t[:, n * BT:(n + 1) * BT, :], x1[:, n * BT:(n + 1) * BT, :]).then_inc(stored, 16)
            sp.wait_ge(stored, 16 * NBLK)

        @block.gpsimd
        def _(pool):
            for p in range(NBUF):
                pool.memset(Ks[p][:, :, :].bitcast(F32), 0.0).then_inc(zeroed, 1)
                pool.memset(Qs[p][:, :, :].bitcast(F32), 0.0).then_inc(zeroed, 1)
            pool.memset(zrow[:, :], 0.0).then_inc(zeroed, 1)
            pool.memset(neg_half[:, :], -0.5).then_inc(zeroed, 1)
            pool.memset(ones_w[:, :], 1.0).then_inc(zeroed, 1)
            pool.wait_ge(zeroed, 2 * NBUF + 3)
            for p in range(NBUF):
                pool.memset(Vs[p][:, :, :, :], 0.0).then_inc(zeroed, 1)
            for b in range(B):
                pool.wait_ge(ln_eps, b + 1)
                r = slice(b * KT, (b + 1) * KT)
                pool.tensor_tensor(rstd[:, r], veps[:, r], neg_half[:, r], ALU.pow).then_inc(ln_rstd, 1)
            pool.wait_ge(zeroed, N_ZEROED)
            for p in range(NBUF):
                pool.memset(Vs[p][:, :, :, D:D + 1], 1.0).then_inc(zeroed, 1)
            pool.wait_ge(zeroed, N_ZEROED + NBUF)

            def cut(n, w):
                k = 2 * n + w
                part = (q_part, k_part)[w]
                pool.wait_ge(part_hi, k + 1)
                wait(pool, part_mid, k - 1)
                wait(pool, part_lo, k - 1)
                pool.tensor_tensor(rest[:, w, :], roped[:, w, :], part[:, 0, n, :], ALU.subtract).then_inc(part_rest, 1)
                pool.wait_ge(part_rest, k + 1)
                pool.wait_ge(part_mid, k + 1)
                pool.tensor_tensor(part[:, 2, n, :], rest[:, w, :], part[:, 1, n, :], ALU.subtract).then_inc(part_lo, 1)

            for n in range(NBLK):
                for w in range(2):
                    cut(n, w)

            pool.wait_ge(mod_ok, N_MOD)
            for b in range(B):
                pool.tensor_tensor(wo_g[:, b, :], wo_sb[:, :], ga_b[:, b, :], ALU.mult).then_inc(gate_ok, 1)
                pool.tensor_tensor(bo_g[:, b, :], bo_sb[:, :], ga_b[:, b, :], ALU.mult).then_inc(gate_ok, 1)

            def stage_v(b, m, p):
                wait(pool, pv_mm, (m - NBUF + 1) * KT)
                pool.tensor_copy(Vs[p][:, :, :, 0:D],
                                 v_all[:, b * KT:(b + 1) * KT, bass.ds((m & (NG - 1)) * (HG * D), HG * D)]
                                 .rearrange("p k (h d) -> p k h d", h=HG)).then_inc(v_staged, 1)

            for b in range(B):
                pool.wait_ge(v_ok, 2 * (b + 1))
                if b == 0:
                    pool.wait_ge(gate_ok, 2 * B)
                    for c in range(B):
                        r = slice(c * KT, (c + 1) * KT)
                        pool.tensor_tensor(x_sb[:, r, :], x_sb[:, r, :],
                                           bo_g[:, c, :].unsqueeze(1).broadcast_to([P, KT, C]), ALU.add).then_inc(xbias_ok, 1)
                by_steps(pool, b * 2 * NG, 2 * NG, lambda m, p, b=b: stage_v(b, m, p))

            for n in range(NBLK):
                pool.wait_ge(eps2, n + 1)
                r = slice(n * BT, (n + 1) * BT)
                pool.tensor_tensor(rstd[:, r], veps[:, r], neg_half[:, r], ALU.pow).then_inc(rstd2, 1)

            pool.wait_ge(in_late, 16 * N_LATE)
            cut_weights(pool, 0, 0, 1)
            cut_weights(pool, 1, 1, 1)
            with pool.Fori(1, E // 2) as pair:
                for p in range(2):
                    cut_weights(pool, pair * 2 + p, p, pair + 1)

        @block.scalar
        def _(act):
            act.wait_ge(in_consts, 16 * N_CONST)
            act.activation(silu_e[:, :], cT_sb[:, :], ACT.Exp, scale=-1.0).then_inc(silu_exp, 1)

            def modulate_h(n):
                b = n // 2
                act.wait_ge(xT_mm, n + 1)
                act.activation(hT[:, n * TB:(n + 1) * TB], bank_o[:, :], ACT.Identity,
                               bias=mod[:, 0, b:b + 1], scale=mod[:, 1, b:b + 1]).then_inc(hT_ok, 1)

            def first_parts(n):
                for w in range(2):
                    part = (q_part, k_part)[w]
                    act.wait_ge(rope_sum, 2 * n + w + 1)
                    act.copy(part[:, 0, n, :], roped[:, w, :]).then_inc(part_hi, 1)
                for w in range(2):
                    part = (q_part, k_part)[w]
                    act.wait_ge(part_rest, 2 * n + w + 1)
                    act.copy(part[:, 1, n, :], rest[:, w, :]).then_inc(part_mid, 1)

            act.wait_ge(mod_ok, 3)
            modulate_h(0)
            for n in range(NBLK):
                if n + 1 < NBLK:
                    modulate_h(n + 1)
                first_parts(n)

            def put_shift(m, q, hh):
                act.wait_ge(shift_tr, m * HG + hh + 1)
                act.copy(Qs[q][SHIFT:SHIFT + NSHIFT, hh, :], shift_psum).then_inc(shift_ok, 1)

            def act_step(n, p, first, last):
                for kt in range(KT):
                    wait(act, pv_mm, n * KT + kt - 1)
                    for hh in range(HG):
                        u = kt * HG + hh
                        act.wait_ge(score_mm, n * UNITS + u + 1)
                        act.activation(prob[:, u % RING, :], bank_s[u % 2][:, :], ACT.Exp,
                                       scale=float(D) ** -0.5).then_inc(exp_ok, 1)
                        if kt == 0 and hh == 0 and not first:
                            put_shift(n, p, HG - 1)
                        if kt == 0 and hh == 1 and not first:
                            act.wait_ge(pv_mm, n * KT)
                            wait(act, o_tr, n - 1)
                            act.copy(oT[:, :], bank_o[:, :]).then_inc(oT_ok, 1)
                        if hh == 0 and kt - 1 in SHIFT_AT and not last:
                            put_shift(n + 1, (p + 1) % NBUF, SHIFT_AT.index(kt - 1))

            for hh in range(HG):
                put_shift(0, 0, hh)
            act_step(0, 0, True, False)
            act_step(1, 1, False, False)
            with act.Fori(0, LOOPS) as i:
                for k in range(2, 2 + NBUF):
                    act_step(i * NBUF + k, k % NBUF, False, False)
            act_step(NSTEP - 2, (NSTEP - 2) % NBUF, False, False)
            act_step(NSTEP - 1, (NSTEP - 1) % NBUF, False, True)
            act.wait_ge(pv_mm, NSTEP * KT)
            act.wait_ge(o_tr, NSTEP - 1)
            act.copy(oT[:, :], bank_o[:, :]).then_inc(oT_ok, 1)

            def out_projection(n):
                act.wait_ge(a_tr, n + 1)
                wait(act, wo_mm, n)
                act.copy(attnT[:, n, :], bank_o[:, :]).then_inc(aT_ok, 1)

            def modulate_h2(n):
                b = n // 2
                act.wait_ge(x2_tr, n + 1)
                wait(act, h2lo_ok, n)
                wait(act, route_mm, n)
                act.activation(h2f[:, n, :], bank_m[0][:, TB:2 * TB], ACT.Identity,
                               bias=mod[:, 3, b:b + 1], scale=mod[:, 4, b:b + 1]).then_inc(h2_ok, 1)
                act.wait_ge(h2_ok, n + 1)
                act.copy(h2_hi[:, n * TB:(n + 1) * TB], h2f[:, n, :]).then_inc(h2hi_ok, 1)

            def route_exp(n):
                act.wait_ge(lmax_ok, n + 1)
                wait(act, comb_ok, n)
                for t in range(BT):
                    act.activation(ext[:, t, 0:E], logit[:, t, :], ACT.Exp,
                                   bias=neg_lmax[:, t:t + 1]).then_inc(rexp_ok, 1)

            act.wait_ge(ext_init, 1)
            for n in range(NBLK):
                out_projection(n)
                modulate_h2(n)
                route_exp(n)
                act.wait_ge(comb_tr, n + 1)
                act.copy(combT[0:3 * E, n * TB:(n + 1) * TB], comb_psum).then_inc(combT_ok, 1)

            def expert_step(e, s, k):
                q = k % 2
                for c in range(ICH):
                    act.wait_ge(h_mm, s * ICH + c + 1)
                    wait(act, gc_ok, (s - 2) * ICH + c + 1)
                    if c == 0 and k % NBLK == 0:
                        act.wait_ge(bias_ok, e + 1)
                    act.activation(g_sb[:, q, c, :], bank_h[c], ACT.Gelu,
                                   bias=bias[k // NBLK][:, c:c + 1]).then_inc(gelu_ok, 1)
                for c in range(ICH):
                    act.wait_ge(gc_ok, s * ICH + c + 1)
                    wait(act, y_mm, s - 1)
                    act.copy(g_hi[:, q, c, :], gc_sb[:, q, c, :]).then_inc(ghi_ok, 1)

            act.wait_ge(in_late, 16 * N_LATE)
            for k in range(2 * NBLK):
                expert_step(k // NBLK, k, k)
            with act.Fori(1, E // 2) as i:
                for k in range(2 * NBLK):
                    expert_step(i * 2 + k // NBLK, i * 2 * NBLK + k, k)

            for n in range(NBLK):
                act.wait_ge(y_mm, E * NBLK)
                wait(act, y_tr, n - 1)
                act.activation(yT[:, n % 2, :], bank_y[n], ACT.Copy, scale=gb_c[:, n // 2:n // 2 + 1]).then_inc(yT_ok, 1)

        @block.vector
        def _(dve):
            dve.memset(ext[:, :, :], -1.0).then_inc(ext_init, 1)
            dve.memset(combT[:, :], 0.0).then_inc(pad_init, 1)
            dve.memset(b2_parts[:, :, :], 0.0).then_inc(pad_init, 1)
            for b in range(B):
                dve.wait_ge(in_x[b], 16)
                for t in range(b * KT, (b + 1) * KT):
                    dve.bn_stats(stats[:, t, :], x_sb[:, t, :]).then_inc(ln_stat, 1)
                dve.wait_ge(ln_stat, (b + 1) * KT)
                for t in range(b * KT, (b + 1) * KT):
                    dve.bn_aggr(mv[:, t, :], stats[:, t, :]).then_inc(ln_mv, 1)
                dve.wait_ge(ln_mv, (b + 1) * KT)
                r = slice(b * KT, (b + 1) * KT)
                dve.tensor_scalar(veps[:, r], mv[:, r, 1], EPS, None, ALU.add).then_inc(ln_eps, 1)

            dve.wait_ge(silu_exp, 1)
            dve.tensor_scalar(silu_d[:, :], silu_e[:, :], 1.0, None, ALU.add).then_inc(silu_step, 1)
            dve.wait_ge(silu_step, 1)
            dve.reciprocal(silu_r[:, :], silu_d[:, :]).then_inc(silu_step, 1)
            dve.wait_ge(silu_step, 2)
            dve.tensor_tensor(silu_c[:, :], silu_r[:, :], cT_sb[:, :], ALU.mult).then_inc(silu_step, 1)
            dve.wait_ge(silu_step, 3)
            dve.wait_ge(zeroed, N_ZEROED)
            for p in range(NBUF):
                dve.memset(Ks[p][SHIFT:SHIFT + NSHIFT, :, :], 1.0).then_inc(ones_ok, 1)
            for b in range(B):
                dve.tensor_scalar(silu_w[:, b, :], ones_w[:, :], silu_c[:, b:b + 1], None, ALU.mult).then_inc(silu_wide, 1)

            dve.wait_ge(mod_mm, 1)
            dve.tensor_copy(mod[:, :, :], bank_s[0][:, 0:6 * B].rearrange("p (j b) -> p j b", b=B)).then_inc(mod_ok, 1)
            dve.wait_ge(mod_ok, 1)
            for j in (1, 4):
                dve.tensor_scalar(mod[:, j, :], mod[:, j, :], 1.0, None, ALU.add).then_inc(mod_ok, 1)
            count = 3
            dve.wait_ge(mod_mm, 2)
            dve.tensor_copy(raw_a[:, :, :], bank_s[1][:, 0:B * C].rearrange("p (b c) -> p b c", b=B)).then_inc(mod_ok, 1)
            dve.wait_ge(mod_ok, 4)
            for raw, s2, mg, gate in ((raw_a[:, :, :], sgn[:, :, :], mag[:, :, :], ga_b[:, :, :]),
                                      (mod[:, 5, :], gsgn[:, :], gmag[:, :], gb_c[:, :])):
                base = 4 if gate.shape[-1] == C else 8
                dve.tensor_scalar(s2, raw, 0.0, 2.0, ALU.is_ge, ALU.mult).then_inc(mod_ok, 1)
                dve.scalar_tensor_tensor(out=mg, in0=raw, scalar=-1.0, in1=raw, op0=ALU.mult, op1=ALU.max).then_inc(mod_ok, 1)
                dve.wait_ge(mod_ok, base + 2)
                dve.tensor_scalar(mg, mg, 0.25, None, ALU.max).then_inc(mod_ok, 1)
                dve.wait_ge(mod_ok, base + 3)
                dve.scalar_tensor_tensor(out=gate, in0=s2, scalar=-1.0, in1=mg, op0=ALU.add, op1=ALU.mult).then_inc(mod_ok, 1)

            def normalise(b):
                dve.wait_ge(ln_rstd, b + 1)
                for t in range(b * KT, (b + 1) * KT):
                    dve.tensor_scalar(xn[:, t, :], x_sb[:, t, :], mv[:, t, 0:1], rstd[:, t:t + 1],
                                      ALU.subtract, ALU.mult).then_inc(ln_done, 1)

            def rope(n):
                half = slice((n % 2) * TB, (n % 2 + 1) * TB)
                for w in range(2):
                    k = 2 * n + w
                    wait(dve, rope_sum, k - 1)
                    dve.wait_ge(qk_mm, 2 * k + 1)
                    dve.scalar_tensor_tensor(out=rope_a[:, w, :], in0=bank_m[w][:, 0:TB], scalar=bqk_sb[:, 2 * w:2 * w + 1],
                                             in1=cos_sb[:, half], op0=ALU.add, op1=ALU.mult).then_inc(rope_half, 1)
                    dve.wait_ge(qk_mm, 2 * k + 2)
                    dve.scalar_tensor_tensor(out=rope_b[:, w, :], in0=bank_m[w][:, TB:2 * TB],
                                             scalar=bqk_sb[:, 2 * w + 1:2 * w + 2],
                                             in1=sin_sb[:, half], op0=ALU.add, op1=ALU.mult).then_inc(rope_half, 1)
                    dve.wait_ge(rope_half, 2 * k + 2)
                    wait(dve, part_hi, k - 1)
                    wait(dve, part_rest, k - 1)
                    dve.tensor_tensor(roped[:, w, :], rope_a[:, w, :], rope_b[:, w, :], ALU.add).then_inc(rope_sum, 1)

            def value_bias(n):
                dve.wait_ge(v_mm, n + 1)
                dve.tensor_tensor(v_all[:, n * BT:(n + 1) * BT, :], bank_x[:, :].rearrange("p (t c) -> p t c", t=BT),
                                  bv_sb[:, :].unsqueeze(1).broadcast_to([P, BT, C]), ALU.add).then_inc(v_ok, 1)

            normalise(0)
            dve.wait_ge(in_rope, 32)
            for n in range(NBLK):
                rope(n)
                if n == 0:
                    normalise(1)
                value_bias(n)

            dve.wait_ge(in_late, 16 * N_LATE)
            dve.wait_ge(pad_init, 2)
            rows = slice(0, 3 * E)
            dve.tensor_copy(b2_parts[rows, 0, :], b2_sb[rows, :]).then_inc(b2_step, 1)
            dve.wait_ge(b2_step, 1)
            dve.tensor_tensor(b2_r[rows, :], b2_sb[rows, :], b2_parts[rows, 0, :], ALU.subtract).then_inc(b2_step, 1)
            dve.wait_ge(b2_step, 2)
            dve.tensor_copy(b2_parts[rows, 1, :], b2_r[rows, :]).then_inc(b2_step, 1)
            dve.wait_ge(b2_step, 3)
            dve.tensor_tensor(b2_parts[rows, 2, :], b2_r[rows, :], b2_parts[rows, 1, :], ALU.subtract).then_inc(b2_step, 1)

            def maxima(m, q, r):
                dve.wait_ge(max_mm, m * MAXU + r + 1)
                wait(dve, shift_lo, (m - NBUF) * HG + r // BT + 1)
                dve.tensor_reduce(neg_max[q][:, r:r + 1], bank_m[r % 2][:, :], AX.X, ALU.max,
                                  negate=True).then_inc(max_ok, 1)
                if r % BT == BT - 1:
                    hh = r // BT
                    cols = slice(hh * BT, (hh + 1) * BT)
                    dve.wait_ge(max_ok, m * MAXU + r + 1)
                    wait(dve, shift_tr, (m - NBUF) * HG + hh + 1)
                    dve.tensor_copy(shift_parts[q][:, cols, 0], neg_max[q][:, cols]).then_inc(shift_hi, 1)
                    dve.wait_ge(shift_hi, m * HG + hh + 1)
                    dve.tensor_tensor(shift_parts[q][:, cols, 1], neg_max[q][:, cols], shift_parts[q][:, cols, 0],
                                      ALU.subtract).then_inc(shift_lo, 1)

            def divide(n, where):
                dve.wait_ge(o_tr, n + 1)
                wait(dve, attn_ok, n)
                o4 = bank_x[:, :].rearrange("p (t h w) -> p t h w", t=BT, h=HG)
                dve.reciprocal(rden[:, :].rearrange("p (t h) -> p t h", t=BT), o4[:, :, :, D]).then_inc(rden_ok, 1)
                dve.wait_ge(rden_ok, n + 1)
                dve.tensor_tensor(where, o4[:, :, :, 0:D],
                                  rden[:, :].rearrange("p (t h) -> p t h", t=BT).unsqueeze(3).broadcast_to([P, BT, HG, D]),
                                  ALU.mult).then_inc(attn_ok, 1)

            attn_g = attn[:, :, :].rearrange("p (n t) c -> p n t c", n=NBLK)

            def attn_at(n):
                return attn_g[:, bass.ds((n & (NSTEP - NG)) >> 2, 1), :, bass.ds((n & (NG - 1)) * (HG * D), HG * D)]\
                    .rearrange("p n t (h d) -> p (n t) h d", h=HG)

            def dve_step(n, p, first, last):
                for r in range(MAXU):
                    if not last:
                        maxima(n + 1, (p + 1) % NBUF, r)
                    if r == 4 and not first:
                        divide(n - 1, attn_at(n - 1))

            for r in range(MAXU):
                maxima(0, 0, r)
            dve_step(0, 0, True, False)
            dve_step(1, 1, False, False)
            with dve.Fori(0, LOOPS) as i:
                for k in range(2, 2 + NBUF):
                    dve_step(i * NBUF + k, k % NBUF, False, False)
            dve_step(NSTEP - 2, (NSTEP - 2) % NBUF, False, False)
            dve_step(NSTEP - 1, (NSTEP - 1) % NBUF, False, True)
            divide(NSTEP - 1, attn_at(NSTEP - 1))

            def residual(n):
                r = slice(n * BT, (n + 1) * BT)
                dve.wait_ge(wo_mm, n + 1)
                dve.wait_ge(xbias_ok, B)
                dve.tensor_tensor(x1[:, r, :], bank_m[0][:, 0:TB].rearrange("p (t c) -> p t c", t=BT), x_sb[:, r, :],
                                  ALU.add).then_inc(x1_ok, 1)
                dve.wait_ge(x1_ok, n + 1)
                for t in range(n * BT, (n + 1) * BT):
                    dve.bn_stats(stats[:, t, :], x1[:, t, :]).then_inc(st2, 1)
                dve.wait_ge(st2, (n + 1) * BT)
                for t in range(n * BT, (n + 1) * BT):
                    dve.bn_aggr(mv[:, t, :], stats[:, t, :]).then_inc(mv2, 1)
                dve.wait_ge(mv2, (n + 1) * BT)
                dve.tensor_scalar(veps[:, r], mv[:, r, 1], EPS, None, ALU.add).then_inc(eps2, 1)
                dve.wait_ge(rstd2, n + 1)
                for t in range(n * BT, (n + 1) * BT):
                    dve.tensor_scalar(xn[:, t, :], x1[:, t, :], mv[:, t, 0:1], rstd[:, t:t + 1],
                                      ALU.subtract, ALU.mult).then_inc(xn2, 1)

            def route(n):
                dve.wait_ge(h2hi_ok, n + 1)
                cols = slice(n * TB, (n + 1) * TB)
                dve.tensor_tensor(h2_lo[:, cols], h2f[:, n, :], h2_hi[:, cols].bitcast(F32), ALU.subtract).then_inc(h2lo_ok, 1)
                dve.wait_ge(route_mm, n + 1)
                wait(dve, rexp_ok, n * BT)
                dve.tensor_tensor(logit[:, :, :], bank_m[1][:, 0:BT * E].rearrange("p (t e) -> p t e", t=BT),
                                  rb_sb[:, 0, :].unsqueeze(1).broadcast_to([P, BT, E]), ALU.add).then_inc(logit_ok, 1)
                dve.wait_ge(logit_ok, n + 1)
                dve.tensor_reduce(neg_lmax[:, :], logit[:, :, :], AX.X, ALU.max, negate=True).then_inc(lmax_ok, 1)
                base = n * N_TOP
                dve.wait_ge(rexp_ok, (n + 1) * BT)
                for t in range(BT):
                    dve.max(top8[:, t, :], ext[:, t, :]).then_inc(top_ok, 1)
                dve.wait_ge(top_ok, base + BT)
                dve.memset(top8[:, :, TOPK:8], -1.0).then_inc(top_ok, 1)
                dve.wait_ge(top_ok, base + BT + 1)
                for t in range(BT):
                    dve.match_replace(marked[:, t, :], top8[:, t, :], ext[:, t, :], -2.0).then_inc(top_ok, 1)
                dve.wait_ge(top_ok, base + 2 * BT + 1)
                dve.scalar_tensor_tensor(out=chosen[:, :, :], in0=marked[:, :, 0:E], scalar=-2.0, in1=ext[:, :, 0:E],
                                         op0=ALU.is_equal, op1=ALU.mult).then_inc(top_ok, 1)
                dve.wait_ge(top_ok, base + 2 * BT + 2)
                dve.tensor_reduce(csum[:, :], chosen[:, :, :], AX.X, ALU.add).then_inc(top_ok, 1)
                dve.wait_ge(top_ok, base + 2 * BT + 3)
                dve.reciprocal(crec[:, :], csum[:, :]).then_inc(top_ok, 1)
                dve.wait_ge(top_ok, base + 2 * BT + 4)
                dve.tensor_tensor(comb[:, :, :], chosen[:, :, :], crec[:, :].unsqueeze(2).broadcast_to([P, BT, E]),
                                  ALU.mult).then_inc(comb_ok, 1)
                dve.wait_ge(comb_ok, n + 1)
                wait(dve, comb_tr, n)
                dve.tensor_copy(comb_parts[:, :, 0, :], comb[:, :, :]).then_inc(top_ok, 1)
                dve.wait_ge(top_ok, base + 2 * BT + 5)
                dve.tensor_tensor(comb_r[:, :, :], comb[:, :, :], comb_parts[:, :, 0, :], ALU.subtract).then_inc(top_ok, 1)
                dve.wait_ge(top_ok, base + 2 * BT + 6)
                dve.tensor_copy(comb_parts[:, :, 1, :], comb_r[:, :, :]).then_inc(top_ok, 1)
                dve.wait_ge(top_ok, base + 2 * BT + 7)
                dve.tensor_tensor(comb_parts[:, :, 2, :], comb_r[:, :, :], comb_parts[:, :, 1, :], ALU.subtract).then_inc(top_ok, 1)

            for n in range(NBLK):
                residual(n)
                route(n)

            def expert_step(s, k):
                q = k % 2
                for c in range(ICH):
                    dve.wait_ge(gelu_ok, s * ICH + c + 1)
                    if c == 0:
                        dve.wait_ge(cb_mm, s + 1)
                    wait(dve, glo_ok, (s - 2) * ICH + c + 1)
                    dve.tensor_tensor(gc_sb[:, q, c, :], g_sb[:, q, c, :], bank_c[q], ALU.mult).then_inc(gc_ok, 1)
                for c in range(ICH):
                    dve.wait_ge(ghi_ok, s * ICH + c + 1)
                    wait(dve, y_mm, s - 1)
                    dve.tensor_tensor(g_lo[:, q, c, :], gc_sb[:, q, c, :], g_hi[:, q, c, :].bitcast(F32),
                                      ALU.subtract).then_inc(glo_ok, 1)

            for k in range(2 * NBLK):
                expert_step(k, k)
            with dve.Fori(1, E // 2) as i:
                for k in range(2 * NBLK):
                    expert_step(i * 2 * NBLK + k, k)

            for n in range(NBLK):
                dve.wait_ge(y_tr, n + 1)
                r = slice(n * BT, (n + 1) * BT)
                dve.tensor_tensor(x1[:, r, :], bank_r[n % 2].rearrange("p (t c) -> p t c", t=BT), x1[:, r, :],
                                  ALU.add).then_inc(out_ok, 1)

        @block.tensor
        def _(pe):
            pe.wait_ge(in_consts, 16 * N_CONST)
            pe.wait_ge(silu_step, 3)
            for j in range(6):
                mm = pe.matmul(bank_s[0][:, j * B:(j + 1) * B], wmod_sb[:, j, :], silu_c[:, :], start=True, stop=True)
            mm.then_inc(mod_mm, 1)
            pe.wait_ge(silu_wide, B)
            for b in range(B):
                mm = pe.matmul(bank_s[1][:, b * C:(b + 1) * C], silu_w[:, b, :], wmod_sb[:, 2, :], start=True, stop=True)
            mm.then_inc(mod_mm, 1)

            def transpose_x(n):
                pe.wait_ge(ln_done, (n + 1) * BT)
                wait(pe, hT_ok, n)
                for t in range(BT):
                    mm = pe.transpose(bank_o[:, t * P:(t + 1) * P], xn[:, n * BT + t, :], id_f[:, :])
                mm.then_inc(xT_mm, 1)

            def project(n):
                cols = slice(n * TB, (n + 1) * TB)
                pe.wait_ge(hT_ok, n + 1)
                for w in range(2):
                    for j in range(2):
                        wait(pe, rope_half, 4 * (n - 1) + 2 * w + j + 1)
                        pe.matmul(bank_m[w][:, j * TB:(j + 1) * TB], wqk_sb[:, 2 * w + j, :], hT[:, cols],
                                  start=True, stop=True).then_inc(qk_mm, 1)
                wait(pe, v_ok, n)
                for t in range(BT):
                    tok = n * TB + t * P
                    mm = pe.matmul(bank_x[:, t * C:(t + 1) * C], hT[:, tok:tok + P], wv_sb[:, :], start=True, stop=True)
                mm.then_inc(v_mm, 1)

            transpose_x(0)
            for n in range(NBLK):
                if n + 1 < NBLK:
                    transpose_x(n + 1)
                project(n)

            def max_unit(m, q, r):
                hh, t = r // BT, r % BT
                wait(pe, max_ok, m * MAXU + r - 1)
                for half in range(2):
                    mm = pe.matmul(bank_m[r % 2][:, half * TB:(half + 1) * TB], Qs[q][:, hh, t * P:(t + 1) * P],
                                   Ks[q][:, hh, half * TB:(half + 1) * TB], start=True, stop=True)
                mm.then_inc(max_mm, 1)

            def turn_shift(m, q, hh):
                pe.wait_ge(shift_lo, m * HG + hh + 1)
                wait(pe, shift_ok, m * HG + hh)
                for t in range(BT):
                    mm = pe.transpose(shift_psum[:, t * P:(t + 1) * P], shift_parts[q][:, hh * BT + t, :], id_b[:, :])
                mm.then_inc(shift_tr, 1)

            def scores(n, p, kt, hh):
                u = kt * HG + hh
                wait(pe, exp_ok, n * UNITS + u - 1)
                if kt == 0:
                    pe.wait_ge(shift_ok, n * HG + hh + 1)
                pe.matmul(bank_s[u % 2][:, :], Ks[p][:, hh, kt * P:(kt + 1) * P], Qs[p][:, hh, :],
                          start=True, stop=True).then_inc(score_mm, 1)

            def products(n, p, kt):
                pe.wait_ge(exp_ok, n * UNITS + (kt + 1) * HG)
                if kt == 0:
                    pe.wait_ge(v_staged, n + 1)
                    wait(pe, oT_ok, n)
                for hh in range(HG):
                    mm = pe.matmul(bank_o[hh * VW:(hh + 1) * VW, :], Vs[p][:, kt, hh, :],
                                   prob[:, (kt * HG + hh) % RING, :], start=(kt == 0), stop=(kt == KT - 1))
                mm.then_inc(pv_mm, 1)

            def turn_sums(n):
                pe.wait_ge(oT_ok, n + 1)
                wait(pe, attn_ok, n)
                for t in range(BT):
                    mm = pe.transpose(bank_x[:, t * P:(t + 1) * P], oT[:, t * P:(t + 1) * P], id_f[:, :])
                mm.then_inc(o_tr, 1)

            def pe_step(n, p, turn, first, last):
                m, q = n + 1, (p + 1) % NBUF
                for kt in range(KT):
                    units = [] if last else list(range(MAX_FROM[kt], MAX_FROM[kt + 1]))
                    scores(n, p, kt, 0)
                    scores(n, p, kt, 1)
                    if kt == 0 and not last:
                        pe.wait_ge(staged[q], (turn + 1) * 48)
                    if len(units) > 1:
                        max_unit(m, q, units.pop(0))
                    if kt == 0 and not first:
                        turn_shift(n, p, HG - 1)
                    scores(n, p, kt, 2)
                    if kt > 0:
                        products(n, p, kt - 1)
                    elif not first:
                        products(n - 1, (p - 1) % NBUF, KT - 1)
                    if len(units) > 1:
                        max_unit(m, q, units.pop(0))
                    scores(n, p, kt, 3)
                    for r in units:
                        max_unit(m, q, r)
                    if kt == 1 and not first:
                        turn_sums(n - 1)
                    if kt in SHIFT_AT and not last:
                        if kt == SHIFT_AT[0]:
                            wait(pe, attn_ok, n)
                        turn_shift(m, q, SHIFT_AT.index(kt))

            pe.wait_ge(rope_half, 4 * NBLK)
            pe.wait_ge(v_ok, NBLK)
            pe.wait_ge(hT_ok, NBLK)
            pe.wait_ge(mod_ok, N_MOD)
            pe.wait_ge(staged[0], 48)
            for r in range(MAXU):
                max_unit(0, 0, r)
                if r % BT == BT - 1 and r > BT:
                    turn_shift(0, 0, r // BT - 1)
            turn_shift(0, 0, HG - 1)
            pe_step(0, 0, 0, True, False)
            pe_step(1, 1, 0, False, False)
            with pe.Fori(0, LOOPS) as i:
                for k in range(2, 2 + NBUF):
                    pe_step(i * NBUF + k, k % NBUF, i + (k + 1) // NBUF, False, False)
            pe_step(NSTEP - 2, (NSTEP - 2) % NBUF, (NSTEP - 1) // NBUF, False, False)
            pe_step(NSTEP - 1, (NSTEP - 1) % NBUF, None, False, True)
            products(NSTEP - 1, (NSTEP - 1) % NBUF, KT - 1)
            turn_sums(NSTEP - 1)

            pe.wait_ge(gate_ok, 2 * B)
            for n in range(NBLK):
                if n == 0:
                    pe.wait_ge(attn_ok, NSTEP)
                for t in range(BT):
                    mm = pe.transpose(bank_o[:, t * P:(t + 1) * P], attn[:, n * BT + t, :], id_f[:, :])
                mm.then_inc(a_tr, 1)
                pe.wait_ge(aT_ok, n + 1)
                for t in range(BT):
                    mm = pe.matmul(bank_m[0][:, t * C:(t + 1) * C], attnT[:, n, t * P:(t + 1) * P], wo_g[:, n // 2, :],
                                   start=True, stop=True)
                mm.then_inc(wo_mm, 1)
                pe.wait_ge(xn2, (n + 1) * BT)
                for t in range(BT):
                    mm = pe.transpose(bank_m[0][:, TB + t * P:TB + (t + 1) * P], xn[:, n * BT + t, :], id_f[:, :])
                mm.then_inc(x2_tr, 1)
                pe.wait_ge(h2_ok, n + 1)
                for t in range(BT):
                    mm = pe.matmul(bank_m[1][:, t * E:(t + 1) * E], h2f[:, n, t * P:(t + 1) * P], rw_sb[:, :],
                                   start=True, stop=True)
                mm.then_inc(route_mm, 1)
                pe.wait_ge(top_ok, (n + 1) * N_TOP)
                for t in range(BT):
                    mm = pe.transpose(comb_psum[:, t * P:(t + 1) * P],
                                      comb_parts[:, t, :, :].rearrange("p a e -> p (a e)"), id_b[:, :])
                mm.then_inc(comb_tr, 1)
                pe.wait_ge(combT_ok, n + 1)

            pe.wait_ge(b2_step, 4)
            for n in range(NBLK):
                for i in range(3):
                    pe.matmul(bank_y[n], b2_parts[:, i, :], combT[:, n * TB:(n + 1) * TB], start=(i == 0), stop=False,
                              skip_group_check=True)

            def expert_hidden(e, s, k):
                n, p, q = k % NBLK, k // NBLK, k % 2
                cols = slice(n * TB, (n + 1) * TB)
                if n == 0:
                    pe.wait_ge(w_lo_ok, e + 1)
                wait(pe, gc_ok, (s - 1) * ICH)
                pe.matmul(bank_c[q], select_sb[:, bass.ds(e, 1), :].rearrange("k e m -> k (e m)"), combT[:, cols],
                          start=True, stop=True).then_inc(cb_mm, 1)
                for c in range(ICH):
                    part = slice(c * P, (c + 1) * P)
                    wait(pe, gelu_ok, (s - 1) * ICH + c + 1)
                    pe.matmul(bank_h[c], w_hi[p][:, 0, part], h2_hi[:, cols], start=True, stop=False)
                    pe.matmul(bank_h[c], w_hi[p][:, 0, part], h2_lo[:, cols], start=False, stop=False)
                    pe.matmul(bank_h[c], w_lo[p][:, 0, part], h2_hi[:, cols], start=False, stop=True).then_inc(h_mm, 1)

            def expert_sum(s, k):
                n, p, q = k % NBLK, k // NBLK, k % 2
                for c in range(ICH):
                    part = slice(c * C, (c + 1) * C)
                    pe.wait_ge(ghi_ok, s * ICH + c + 1)
                    pe.matmul(bank_y[n], w_hi[p][:, 1, part], g_hi[:, q, c, :], start=False, stop=False, skip_group_check=True)
                    pe.matmul(bank_y[n], w_lo[p][:, 1, part], g_hi[:, q, c, :], start=False, stop=False, skip_group_check=True)
                    pe.wait_ge(glo_ok, s * ICH + c + 1)
                    mm = pe.matmul(bank_y[n], w_hi[p][:, 1, part], g_lo[:, q, c, :], start=False, stop=True, skip_group_check=True)
                mm.then_inc(y_mm, 1)

            LAST = 2 * NBLK - 1
            pe.wait_ge(h2lo_ok, NBLK)
            expert_hidden(0, 0, 0)
            for k in range(LAST):
                expert_hidden((k + 1) // NBLK, k + 1, k + 1)
                expert_sum(k, k)
            with pe.Fori(1, E // 2) as i:
                for k in range(-1, LAST):
                    expert_hidden(i * 2 + (k + 1) // NBLK, i * 2 * NBLK + k + 1, k + 1)
                    expert_sum(i * 2 * NBLK + k, k % (2 * NBLK))
            expert_sum(E * NBLK - 1, LAST)

            for n in range(NBLK):
                pe.wait_ge(yT_ok, n + 1)
                wait(pe, out_ok, n - 1)
                for t in range(BT):
                    mm = pe.transpose(bank_r[n % 2][:, t * P:(t + 1) * P], yT[:, n % 2, t * P:(t + 1) * P], id_f[:, :])
                mm.then_inc(y_tr, 1)


def kernel(L0_attn_x, L0_attn_Wq, L0_attn_bq, L0_attn_Wk, L0_attn_bk, L0_attn_Wv, L0_attn_bv, L0_attn_Wo, L0_attn_bo,
           L0_ffn_router_w, L0_ffn_router_b, L0_ffn_w1, L0_ffn_b1, L0_ffn_w2, L0_ffn_b2, L0_c, L0_wmod):
    import numpy as np
    import concourse.bacc as bacc
    from concourse.bass_utils import run_bass_kernel_spmd

    f32 = np.float32
    swap = np.arange(H * D).reshape(H, 2, D // 2)[:, ::-1].reshape(-1)
    theta = f32(10000.0) ** (-np.arange(D // 2, dtype=f32) / f32(D // 2))
    angle = np.arange(T, dtype=f32)[:, None] * theta[None, :]
    cos = np.tile(np.cos(angle).T, (2 * H, 1)).astype(f32)
    sin = np.tile(np.concatenate([-np.sin(angle).T, np.sin(angle).T]), (H, 1)).astype(f32)
    row = np.arange(P)
    select = ((row[:, None] % E == np.arange(E)[None, :]) & (row[:, None] < 3 * E))
    select = np.repeat(select[:, :, None], P, axis=2).reshape(P, E * P)
    bf16 = mybir.dt.np(BF16)
    wq, wk = np.asarray(L0_attn_Wq), np.asarray(L0_attn_Wk)
    bq, bk = np.asarray(L0_attn_bq), np.asarray(L0_attn_bk)
    arrays = {
        "x": np.asarray(L0_attn_x),
        "wqkT": np.stack([wq.T, wq[swap].T, wk.T, wk[swap].T]),
        "bqk": np.stack([bq, bq[swap], bk, bk[swap]], axis=1),
        "wvT": np.asarray(L0_attn_Wv).T,
        "bv": np.asarray(L0_attn_bv),
        "woT": np.asarray(L0_attn_Wo).T,
        "bo": np.asarray(L0_attn_bo),
        "router_w": np.asarray(L0_ffn_router_w),
        "router_b": np.asarray(L0_ffn_router_b),
        "w1": np.asarray(L0_ffn_w1),
        "b1T": np.asarray(L0_ffn_b1).reshape(E * ICH, P).T,
        "w2": np.asarray(L0_ffn_w2),
        "b2": np.asarray(L0_ffn_b2),
        "cT": np.asarray(L0_c).T,
        "wmod": np.asarray(L0_wmod),
        "cos": cos,
        "sin": sin,
        "ident": np.eye(P, dtype=f32),
        "identb": np.eye(P).astype(bf16),
        "select": select.astype(bf16),
    }
    nc = bacc.Bacc("TRN2", target_bir_lowering=False, num_devices=1)
    feeds, args = {}, []
    for name, a in arrays.items():
        a = np.ascontiguousarray(a)
        feeds[f"in_{name}"] = a
        args.append(nc.dram_tensor(f"in_{name}", a.shape, mybir.dt.from_np(a.dtype), kind="ExternalInput").ap())
    args.append(nc.dram_tensor("out_dram", (B, T, C), F32, kind="ExternalOutput").ap())
    block_program(nc, *args)
    r = run_bass_kernel_spmd(nc, [feeds], core_ids=[0])
    return r.results[0]["out_dram"]
```

```python
from contextlib import ExitStack

import concourse.bass as bass
from concourse import mybir

F32 = mybir.dt.float32
F32R = mybir.dt.float32r
BF16 = mybir.dt.bfloat16
ALU = mybir.AluOpType
ACT = mybir.ActivationFunctionType
AX = mybir.AxisListType

P = 128
B, T, C = 2, 1024, 128
H, D = 16, 8
E, I = 16, 256
TOPK = 4
TB = 512
NBLK = B * T // TB
NT = B * T // P
BT = TB // P
HG = 4
NG = H // HG
KT = T // P
NSTEP = NBLK * NG
VW = 32
TERMS = 6
ROWS = D * TERMS
SHIFT = 64
NSHIFT = 2
UNITS = KT * HG
MAXU = HG * BT
RING = 8
NBUF = 3
Q_ROWS = (slice(0, 5, 2), slice(1, 4, 2), slice(5, 6))
K_ROWS = (slice(3, 6), slice(0, 2), slice(2, 3))
ICH = I // P
EPS = 1e-5
LOOPS = (NSTEP - 4) // NBUF
SHIFT_AT = (3, 5, 6)


def block_program(nc: bass.Bass, x, wqkT, bqk, wvT, bv, woT, bo, router_w, router_b, w1, b1T, w2, b2,
                  cT, wmod, cos, sin, ident, identb, select, out):
    ctx = ExitStack()
    with ctx:
        def sb(name, shape, dt=F32):
            return ctx.enter_context(nc.sbuf_tensor(name, shape, dt))

        projecting = ExitStack()

        def sbp(name, shape, dt=F32):
            return projecting.enter_context(nc.sbuf_tensor(name, shape, dt))

        passing = ExitStack()

        def sba(name, shape, dt=F32):
            return passing.enter_context(nc.sbuf_tensor(name, shape, dt))

        def psum(name, shape, dt=F32):
            return ctx.enter_context(nc.psum_tensor(name, shape, dt))

        def sem(name):
            return ctx.enter_context(nc.semaphore(name))

        q_rows = nc.dram_tensor("q_rows", [NBLK, H * D, TERMS, TB], BF16, kind="Internal").ap()
        k_rows = nc.dram_tensor("k_rows", [B, H * D, TERMS, T], BF16, kind="Internal").ap()

        x_sb = sb("x_sb", [P, NT, C])
        xn = sb("xn", [P, NT, C])
        id_f = sb("id_f", [P, P])
        id_b = sb("id_b", [P, P], BF16)
        wqk_sb = sb("wqk_sb", [P, 4, C])
        bqk_sb = sb("bqk_sb", [P, 4])
        wv_sb = sb("wv_sb", [P, C])
        bv_sb = sb("bv_sb", [P, C])
        wo_sb = sb("wo_sb", [P, C])
        wo_g = sb("wo_g", [P, B, C])
        bo_sb = sb("bo_sb", [P, C])
        bo_g = sb("bo_g", [P, B, C])
        cT_sb = sb("cT_sb", [P, B])
        silu_e = sb("silu_e", [P, B])
        silu_d = sb("silu_d", [P, B])
        silu_r = sb("silu_r", [P, B])
        silu_c = sb("silu_c", [P, B])
        silu_w = sb("silu_w", [P, B, P])
        ones_w = sb("ones_w", [P, P])
        wmod_sb = sb("wmod_sb", [P, 6, C])
        mod = sb("mod", [P, 6, B])
        raw_a = sb("raw_a", [P, B, C])
        sgn = sb("sgn", [P, B, C])
        mag = sb("mag", [P, B, C])
        ga_b = sb("ga_b", [P, B, C])
        gsgn = sb("gsgn", [P, B])
        gmag = sb("gmag", [P, B])
        gb_c = sb("gb_c", [P, B])
        stats = sb("stats", [P, NT, 6])
        mv = sb("mv", [P, NT, 2])
        veps = sb("veps", [P, NT])
        neg_half = sb("neg_half", [P, NT])
        rstd = sb("rstd", [P, NT])
        neg_max = [sb(f"neg_max{i}", [P, MAXU]) for i in range(NBUF)]
        shift_parts = [sb(f"shift_parts{i}", [P, MAXU, NSHIFT], BF16) for i in range(NBUF)]
        rden = sb("rden", [P, BT * HG])
        attn = sb("attn", [P, NT, C])
        rw_sb = sb("rw_sb", [P, E])
        rb_sb = sb("rb_sb", [P, E])
        logit = sb("logit", [P, NT, E])
        neg_lmax = sb("neg_lmax", [P, NT])
        ext = sb("ext", [P, NT, E + TOPK])
        top8 = sb("top8", [P, NT, 8])
        marked = sb("marked", [P, NT, E + TOPK])
        chosen = sb("chosen", [P, NT, E])
        csum = sb("csum", [P, NT])
        crec = sb("crec", [P, NT])
        shifted = sb("shifted", [P, NT, E])
        comb = sb("comb", [P, NT, E])
        comb_r = sb("comb_r", [P, NT, E])
        comb_parts = sb("comb_parts", [P, NT, 3, E], BF16)
        combT = sb("combT", [P, B * T], BF16)
        select_sb = sb("select_sb", [P, E, P], BF16)
        b2_sb = sb("b2_sb", [3 * E, C])
        b2_r = sb("b2_r", [3 * E, C])
        b2_parts = sb("b2_parts", [P, 3, C], BF16)
        b1_sb = sb("b1_sb", [P, E * ICH])
        hT = sbp("hT", [P, B * T])
        cos_sb = sbp("cos_sb", [P, T])
        sin_sb = sbp("sin_sb", [P, T])
        rope_a = sbp("rope_a", [P, 2, TB])
        rope_b = sbp("rope_b", [P, 2, TB])
        roped = sbp("roped", [P, 2, 2, TB])
        rest = sbp("rest", [P, 2, 2, TB])
        projecting.close()
        x1 = sb("x1", [P, NT, C])
        attnT = sb("attnT", [P, NBLK, TB])
        h2f = sb("h2f", [P, NBLK, TB])
        h2_hi = sb("h2_hi", [P, B * T], F32R)
        h2_lo = sb("h2_lo", [P, B * T], F32R)
        q_part = sba("q_part", [P, 3, NBLK, TB], BF16)
        k_part = sba("k_part", [P, 3, NBLK, TB], BF16)
        v_all = sba("v_all", [P, NT, H * D])
        Qs = [sba(f"Qs{i}", [P, HG, TB], BF16) for i in range(NBUF)]
        Ks = [sba(f"Ks{i}", [P, HG, T], BF16) for i in range(NBUF)]
        Vs = [sba(f"Vs{i}", [P, KT, HG, VW]) for i in range(NBUF)]
        ones_row = sba("ones_row", [NSHIFT, T], BF16)
        zrow = sba("zrow", [NSHIFT, HG * TB], BF16)
        prob = sba("prob", [P, RING, TB])
        oT = sba("oT", [P, TB])
        passing.close()
        bias = [sb(f"bias{i}", [P, ICH]) for i in range(2)]
        w_st = [sb(f"w_st{i}", [P, 2, I]) for i in range(2)]
        w_hi = [sb(f"w_hi{i}", [P, 2, I], F32R) for i in range(2)]
        w_lo = [sb(f"w_lo{i}", [P, 2, I], F32R) for i in range(2)]
        g_sb = sb("g_sb", [P, 2, ICH, TB])
        gc_sb = sb("gc_sb", [P, 2, ICH, TB])
        g_hi = sb("g_hi", [P, 2, ICH, TB], F32R)
        g_lo = sb("g_lo", [P, 2, ICH, TB], F32R)
        yT = sb("yT", [P, 2, TB])

        bank_s = [psum(f"bank_s{i}", [P, TB]) for i in range(2)]
        bank_m = [psum(f"bank_m{i}", [P, 2 * TB]) for i in range(2)]
        bank_o = psum("bank_o", [P, TB])
        bank_x = psum("bank_x", [P, TB])

        shift_psum = bank_x[:, :].bitcast(BF16)[SHIFT:SHIFT + NSHIFT, 0:TB]
        bank_w = [bank_m[0][:, 0:TB], bank_m[0][:, TB:2 * TB], bank_m[1][:, 0:TB], bank_x[:, :]]
        bank_e = [bank_s[0][:, :], bank_s[1][:, :]]
        bank_e_last = bank_e + [bank_m[1][:, TB:2 * TB]]
        bank_y = [bank_s[0][:, :], bank_s[1][:, :], bank_o[:, :], bank_x[:, :]]
        bank_h = [bank_m[0][:, 0:TB], bank_m[0][:, TB:2 * TB]]
        bank_c = [bank_m[1][:, 0:TB], bank_m[1][:, TB:2 * TB]]

        in_mod = sem("in_mod")
        in_proj = sem("in_proj")
        in_consts = sem("in_consts")
        in_x = [sem(f"in_x{b}") for b in range(B)]
        in_rope = sem("in_rope")
        in_late = sem("in_late")
        zeroed = sem("zeroed")
        const_ok = sem("const_ok")
        ones_ok = sem("ones_ok")
        vones_ok = sem("vones_ok")
        silu_exp = sem("silu_exp")
        silu_step = sem("silu_step")
        silu_wide = sem("silu_wide")
        mod_mm = sem("mod_mm")
        mod_ok = sem("mod_ok")
        gate_ok = sem("gate_ok")
        ln_stat = sem("ln_stat")
        ln_mv = sem("ln_mv")
        ln_eps = sem("ln_eps")
        ln_rstd = sem("ln_rstd")
        ln_done = sem("ln_done")
        xT_mm = sem("xT_mm")
        hT_ok = sem("hT_ok")
        qk_mm = sem("qk_mm")
        rope_half = sem("rope_half")
        rope_sum = sem("rope_sum")
        part_hi = sem("part_hi")
        part_rest = sem("part_rest")
        part_mid = sem("part_mid")
        part_lo = sem("part_lo")
        v_mm = sem("v_mm")
        v_ok = sem("v_ok")
        rows_out = sem("rows_out")
        staged = [sem(f"staged{i}") for i in range(NBUF)]
        v_staged = sem("v_staged")
        max_mm = sem("max_mm")
        max_ok = sem("max_ok")
        shift_hi = sem("shift_hi")
        shift_lo = sem("shift_lo")
        shift_tr = sem("shift_tr")
        shift_ok = sem("shift_ok")
        score_mm = sem("score_mm")
        exp_ok = sem("exp_ok")
        pv_mm = sem("pv_mm")
        oT_ok = sem("oT_ok")
        o_tr = sem("o_tr")
        rden_ok = sem("rden_ok")
        attn_ok = sem("attn_ok")
        a_tr = sem("a_tr")
        aT_ok = sem("aT_ok")
        wo_mm = sem("wo_mm")
        x1_ok = sem("x1_ok")
        xbias_ok = sem("xbias_ok")
        st2 = sem("st2")
        mv2 = sem("mv2")
        eps2 = sem("eps2")
        rstd2 = sem("rstd2")
        xn2 = sem("xn2")
        x2_tr = sem("x2_tr")
        h2_ok = sem("h2_ok")
        h2hi_ok = sem("h2hi_ok")
        h2lo_ok = sem("h2lo_ok")
        route_mm = sem("route_mm")
        logit_ok = sem("logit_ok")
        lmax_ok = sem("lmax_ok")
        rexp_ok = sem("rexp_ok")
        ext_init = sem("ext_init")
        pad_init = sem("pad_init")
        top_ok = sem("top_ok")
        comb_ok = sem("comb_ok")
        comb_tr = sem("comb_tr")
        combT_ok = sem("combT_ok")
        b2_step = sem("b2_step")
        w_in = [sem(f"w_in{i}") for i in range(2)]
        bias_ok = sem("bias_ok")
        w_hi_ok = sem("w_hi_ok")
        w_lo_ok = sem("w_lo_ok")
        cb_mm = sem("cb_mm")
        h_mm = sem("h_mm")
        gelu_ok = sem("gelu_ok")
        gc_ok = sem("gc_ok")
        ghi_ok = sem("ghi_ok")
        glo_ok = sem("glo_ok")
        y_mm = sem("y_mm")
        yT_ok = sem("yT_ok")
        y_tr = sem("y_tr")
        out_ok = sem("out_ok")
        stored = sem("stored")

        N_MOD = 12
        GROUPS = (range(0, NBLK - 1), range(NBLK - 1, NBLK))
        TOP_BASE = (0, 2 * (NBLK - 1) * BT + 8, 2 * NBLK * BT + 16)
        N_MODIN, N_PROJ, N_CONST, N_LATE = 2, 5, 5, 5
        N_ZEROED = 3 * NBUF + 2

        REGULAR = [(p, n) for p in range(2) for n in range(NBLK)]
        BEGINNING = [(0, n) for n in range(NBLK - 1)] + [(1, n) for n in range(NBLK - 2)] \
            + [(0, NBLK - 1), (1, NBLK - 2), (1, NBLK - 1)]

        def wait(eng, s, value):
            if isinstance(value, int) and value <= 0:
                return
            eng.wait_ge(s, value)

        N_STORES = 3 * (1 + 2)

        def by_steps(eng, first, count, body, begun=False):
            lone = range(first, first + 2) if first == 0 else range(first + count - 2, first + count)
            rest = [m for m in range(first, first + count) if m not in lone]
            if first == 0:
                for m in lone[begun:]:
                    body(m, m % NBUF)
            with eng.Fori(0, len(rest) // NBUF) as i:
                for k in range(NBUF):
                    body(i * NBUF + (rest[0] + k), (rest[0] + k) % NBUF)
            if first != 0:
                for m in lone:
                    body(m, m % NBUF)

        def stage(sp, b, m, p):
            wait(sp, score_mm, (m - NBUF + 1) * UNITS)
            heads = bass.ds((m & (NG - 1)) * (HG * D), HG * D)
            sp.dma_start(Qs[p][0:ROWS, :, :], q_rows.rearrange("n r e t -> (n r) e t")[bass.ds(m * (HG * D), HG * D), :, :]
                         .rearrange("(h d) e t -> (d e) h t", h=HG)).then_inc(staged[p], 16)
            sp.dma_start(Ks[p][0:ROWS, :, :], k_rows[b, heads, :, :]
                         .rearrange("(h d) e t -> (d e) h t", h=HG)).then_inc(staged[p], 16)
            sp.dma_start(Qs[p][SHIFT:SHIFT + NSHIFT, :, :],
                         zrow[:, :].rearrange("p (h t) -> p h t", h=HG)).then_inc(staged[p], 16)

        def load_weights(sp, e, p):
            wait(sp, w_lo_ok, (e - 1) * 2)
            sp.dma_start(w_st[p][:, 0, :],
                         w1[bass.ds(e, 1), :, :].rearrange("e c i -> (e c) i")).then_inc(w_in[p], 16)
            sp.dma_start(w_st[p][:, 1, :].rearrange("p (h c) -> p h c", h=ICH),
                         w2[bass.ds(e, 1), :, :].rearrange("e (h p) c -> p (e h) c", h=ICH)).then_inc(w_in[p], 16)

        def cut_weights(pool, e, p, nth, used):
            pool.wait_ge(w_in[p], nth * 32)
            wait(pool, y_mm, used)
            pool.tensor_tensor(bias[p][:, :], b1_sb[:, bass.ds(e * ICH, ICH)], ones_w[:, 0:ICH],
                               ALU.mult).then_inc(bias_ok, 1)
            for w in range(2):
                pool.tensor_tensor(w_hi[p][:, w, :], w_st[p][:, w, :],
                                   ones_w[:, 0:1].broadcast_to([P, I]), ALU.mult).then_inc(w_hi_ok, 1)
                pool.wait_ge(w_hi_ok, e * 2 + (w + 1))
                pool.tensor_tensor(w_lo[p][:, w, :], w_st[p][:, w, :], w_hi[p][:, w, :].bitcast(F32),
                                   ALU.subtract).then_inc(w_lo_ok, 1)

        block = ctx.enter_context(nc.Block())

        @block.sync
        def _(sp):
            x_t = x.rearrange("b (n p) c -> p (b n) c", p=P)
            sp.dma_start(x_sb[:, 0:KT, :], x_t[:, 0:KT, :]).then_inc(in_x[0], 16)
            sp.dma_start(cT_sb[:, :], cT).then_inc(in_mod, 16)
            sp.dma_start(wmod_sb[:, :, :], wmod.rearrange("k (j c) -> k j c", j=6)).then_inc(in_mod, 16)
            sp.dma_start(id_f[:, :], ident).then_inc(in_proj, 16)
            sp.dma_start(wqk_sb[:, :, :], wqkT.rearrange("j c o -> c j o")).then_inc(in_proj, 16)
            sp.dma_start(bqk_sb[:, :], bqk).then_inc(in_proj, 16)
            sp.dma_start(cos_sb[:, :], cos).then_inc(in_rope, 16)
            sp.dma_start(sin_sb[:, :], sin).then_inc(in_rope, 16)
            sp.dma_start(wv_sb[:, :], wvT).then_inc(in_proj, 16)
            sp.dma_start(bv_sb[:, :], bv.partition_broadcast(P)).then_inc(in_proj, 16)
            sp.dma_start(x_sb[:, KT:2 * KT, :], x_t[:, KT:2 * KT, :]).then_inc(in_x[1], 16)
            sp.dma_start(id_b[:, :], identb).then_inc(in_consts, 16)
            sp.dma_start(wo_sb[:, :], woT).then_inc(in_consts, 16)
            sp.dma_start(bo_sb[:, :], bo.partition_broadcast(P)).then_inc(in_consts, 16)
            sp.dma_start(rw_sb[:, :], router_w).then_inc(in_consts, 16)
            sp.dma_start(rb_sb[:, :], router_b.partition_broadcast(P)).then_inc(in_consts, 16)
            sp.wait_ge(zeroed, N_ZEROED)
            for p in range(NBUF):
                for hh in range(HG):
                    sp.dma_start(Ks[p][SHIFT:SHIFT + NSHIFT, hh, :], ones_row[:, :]).then_inc(ones_ok, 16)

            sp.dma_start(b1_sb[:, :], b1T).then_inc(in_late, 16)
            for i in range(3):
                sp.dma_start(b2_sb[i * E:(i + 1) * E, :], b2).then_inc(in_late, 16)
            sp.dma_start(select_sb[:, :, :], select.rearrange("k (e m) -> k e m", e=E)).then_inc(in_late, 16)

            for b in range(B):
                sp.wait_ge(part_hi, 4 * (b + 1))
                sp.wait_ge(part_mid, 4 * (b + 1))
                sp.wait_ge(part_lo, 4 * (b + 1))
                for heads in ((slice(0, HG * D), slice(HG * D, H * D)) if b == 0 else (slice(0, H * D),)):
                    for part in range(3):
                        terms = len(range(TERMS)[K_ROWS[part]])
                        sp.dma_start(k_rows[b, heads, K_ROWS[part], :],
                                     k_part[heads, part, 2 * b:2 * b + 2, :].rearrange("p j t -> p (j t)")
                                     .unsqueeze(1).broadcast_to([heads.stop - heads.start, terms, T])).then_inc(rows_out, 16)
                        terms = len(range(TERMS)[Q_ROWS[part]])
                        for j in range(2):
                            sp.dma_start(q_rows[2 * b + j, heads, Q_ROWS[part], :],
                                         q_part[heads, part, 2 * b + j, :]
                                         .unsqueeze(1).broadcast_to([heads.stop - heads.start, terms, TB])).then_inc(rows_out, 16)
                    if b == 0 and heads.start == 0:
                        sp.wait_ge(rows_out, 16 * N_STORES)
                        sp.wait_ge(ones_ok, 16 * NBUF * HG)
                        stage(sp, 0, 0, 0)
                sp.wait_ge(rows_out, 16 * N_STORES * (b + 2))
                by_steps(sp, b * 2 * NG, 2 * NG, lambda m, p, b=b: stage(sp, b, m, p), b == 0)
            load_weights(sp, 0, 0)
            load_weights(sp, 1, 1)
            with sp.Fori(1, E // 2) as pair:
                for p in range(2):
                    load_weights(sp, pair * 2 + p, p)

            o_t = out.rearrange("b (n p) c -> p (b n) c", p=P)
            for n in range(NBLK):
                sp.wait_ge(out_ok, n + 1)
                sp.dma_start(o_t[:, n * BT:(n + 1) * BT, :], x1[:, n * BT:(n + 1) * BT, :]).then_inc(stored, 16)
            sp.wait_ge(stored, 16 * NBLK)

        @block.gpsimd
        def _(pool):
            pool.memset(neg_half[:, :], -0.5).then_inc(const_ok, 1)
            pool.memset(ones_w[:, :], 1.0).then_inc(const_ok, 1)
            pool.memset(zrow[:, :], 0.0).then_inc(zeroed, 1)
            pool.memset(ones_row[:, :], 1.0).then_inc(zeroed, 1)
            pool.memset(Ks[0][:, :, :].bitcast(F32), 0.0).then_inc(zeroed, 1)
            pool.memset(Qs[0][:, :, :].bitcast(F32), 0.0).then_inc(zeroed, 1)
            pool.wait_ge(const_ok, 2)
            for b in range(B):
                pool.wait_ge(ln_eps, b + 1)
                r = slice(b * KT, (b + 1) * KT)
                pool.tensor_tensor(rstd[:, r], veps[:, r], neg_half[:, r], ALU.pow).then_inc(ln_rstd, 1)
                if b == 0:
                    pool.memset(Ks[1][:, :, :].bitcast(F32), 0.0).then_inc(zeroed, 1)
                    pool.memset(Qs[1][:, :, :].bitcast(F32), 0.0).then_inc(zeroed, 1)
                    pool.memset(Ks[2][:, :, :].bitcast(F32), 0.0).then_inc(zeroed, 1)
            pool.memset(Qs[2][:, :, :].bitcast(F32), 0.0).then_inc(zeroed, 1)
            for p in range(NBUF):
                pool.memset(Vs[p][:, :, :, :], 0.0).then_inc(zeroed, 1)
            pool.wait_ge(zeroed, N_ZEROED)
            for p in range(NBUF):
                pool.memset(Vs[p][:, :, :, D:D + 1], 1.0).then_inc(vones_ok, 1)
            pool.wait_ge(vones_ok, NBUF)

            def cut(n):
                for w in range(2):
                    k = 2 * n + w
                    part = (q_part, k_part)[w]
                    pool.wait_ge(part_hi, k + 1)
                    wait(pool, part_mid, k - 3)
                    wait(pool, part_lo, k - 3)
                    pool.tensor_tensor(rest[:, n % 2, w, :], roped[:, n % 2, w, :], part[:, 0, n, :],
                                       ALU.subtract).then_inc(part_rest, 1)
                for w in range(2):
                    k = 2 * n + w
                    part = (q_part, k_part)[w]
                    pool.wait_ge(part_rest, k + 1)
                    pool.wait_ge(part_mid, k + 1)
                    pool.tensor_tensor(part[:, 2, n, :], rest[:, n % 2, w, :], part[:, 1, n, :],
                                       ALU.subtract).then_inc(part_lo, 1)

            for n in range(NBLK):
                cut(n)

            def stage_v(b, m, p):
                wait(pool, pv_mm, (m - NBUF + 1) * KT)
                pool.tensor_copy(Vs[p][:, :, :, 0:D],
                                 v_all[:, b * KT:(b + 1) * KT, bass.ds((m & (NG - 1)) * (HG * D), HG * D)]
                                 .rearrange("p k (h d) -> p k h d", h=HG)).then_inc(v_staged, 1)

            for b in range(B):
                pool.wait_ge(v_ok, 2 * (b + 1))
                if b == 1:
                    pool.wait_ge(mod_ok, N_MOD)
                    pool.wait_ge(in_consts, 16 * N_CONST)
                    for c in range(B):
                        pool.tensor_tensor(wo_g[:, c, :], wo_sb[:, :], ga_b[:, c, :], ALU.mult).then_inc(gate_ok, 1)
                        pool.tensor_tensor(bo_g[:, c, :], bo_sb[:, :], ga_b[:, c, :], ALU.mult).then_inc(gate_ok, 1)
                    pool.wait_ge(gate_ok, 2 * B)
                    for c in range(B):
                        r = slice(c * KT, (c + 1) * KT)
                        pool.tensor_tensor(x_sb[:, r, :], x_sb[:, r, :],
                                           bo_g[:, c, :].unsqueeze(1).broadcast_to([P, KT, C]), ALU.add).then_inc(xbias_ok, 1)
                by_steps(pool, b * 2 * NG, 2 * NG, lambda m, p, b=b: stage_v(b, m, p))

            pool.wait_ge(in_late, 16 * N_LATE)
            cut_weights(pool, 0, 0, 1, 0)
            cut_weights(pool, 1, 1, 1, 0)

            for gi, blocks in enumerate(GROUPS):
                pool.wait_ge(eps2, gi + 1)
                r = slice(blocks[0] * BT, (blocks[-1] + 1) * BT)
                pool.tensor_tensor(rstd[:, r], veps[:, r], neg_half[:, r], ALU.pow).then_inc(rstd2, 1)

            for p in range(2):
                cut_weights(pool, 2 + p, p, 2, BEGINNING.index((p, NBLK - 1)) + 1)
            with pool.Fori(2, E // 2) as pair:
                for p in range(2):
                    cut_weights(pool, pair * 2 + p, p, pair + 1, (pair * 2 + p - 1) * NBLK)

        @block.scalar
        def _(act):
            act.wait_ge(in_mod, 16 * N_MODIN)
            act.activation(silu_e[:, :], cT_sb[:, :], ACT.Exp, scale=-1.0).then_inc(silu_exp, 1)

            def modulate_h(n):
                b = n // 2
                act.wait_ge(xT_mm, n + 1)
                act.activation(hT[:, n * TB:(n + 1) * TB], bank_o[:, :], ACT.Identity,
                               bias=mod[:, 0, b:b + 1], scale=mod[:, 1, b:b + 1]).then_inc(hT_ok, 1)

            def first_parts(n):
                for w in range(2):
                    part = (q_part, k_part)[w]
                    act.wait_ge(rope_sum, 2 * n + w + 1)
                    act.copy(part[:, 0, n, :], roped[:, n % 2, w, :]).then_inc(part_hi, 1)

            def middle_parts(n):
                for w in range(2):
                    part = (q_part, k_part)[w]
                    act.wait_ge(part_rest, 2 * n + w + 1)
                    act.copy(part[:, 1, n, :], rest[:, n % 2, w, :]).then_inc(part_mid, 1)

            act.wait_ge(mod_ok, 3)
            modulate_h(0)
            modulate_h(1)
            first_parts(0)
            middle_parts(0)
            modulate_h(2)
            first_parts(1)
            modulate_h(3)
            middle_parts(1)
            first_parts(2)
            middle_parts(2)
            first_parts(3)
            middle_parts(3)

            def put_shift(m, q, hh):
                act.wait_ge(shift_tr, m * HG + hh + 1)
                act.copy(Qs[q][SHIFT:SHIFT + NSHIFT, hh, :], shift_psum).then_inc(shift_ok, 1)

            def act_step(n, p, first, last):
                banks = bank_e_last if last else bank_e
                for kt in range(KT):
                    wait(act, pv_mm, n * KT + kt - 1)
                    for hh in range(HG):
                        u = kt * HG + hh
                        act.wait_ge(score_mm, n * UNITS + u + 1)
                        act.activation(prob[:, u % RING, :], banks[u % len(banks)], ACT.Exp,
                                       scale=float(D) ** -0.5).then_inc(exp_ok, 1)
                        if kt == 0 and hh == 2 and not first:
                            put_shift(n, p, HG - 1)
                            act.wait_ge(pv_mm, n * KT)
                            wait(act, o_tr, n - 1)
                            act.copy(oT[:, :], bank_o[:, :]).then_inc(oT_ok, 1)
                        if hh == 0 and kt - 1 in SHIFT_AT and not last:
                            put_shift(n + 1, (p + 1) % NBUF, SHIFT_AT.index(kt - 1))

            def out_projection(n):
                act.wait_ge(a_tr, n + 1)
                act.copy(attnT[:, n, :], bank_w[n]).then_inc(aT_ok, 1)

            def modulate_h2(n):
                b = n // 2
                act.wait_ge(x2_tr, n + 1)
                act.activation(h2f[:, n, :], bank_w[n], ACT.Identity,
                               bias=mod[:, 3, b:b + 1], scale=mod[:, 4, b:b + 1]).then_inc(h2_ok, 1)
                act.wait_ge(h2_ok, n + 1)
                act.copy(h2_hi[:, n * TB:(n + 1) * TB], h2f[:, n, :]).then_inc(h2hi_ok, 1)

            def route_exp(gi):
                r = slice(GROUPS[gi][0] * BT, (GROUPS[gi][-1] + 1) * BT)
                act.wait_ge(lmax_ok, 2 * (gi + 1))
                act.activation(ext[:, r, 0:E], shifted[:, r, :], ACT.Exp).then_inc(rexp_ok, 1)

            act.wait_ge(ext_init, 1)
            for hh in range(HG):
                put_shift(0, 0, hh)
            act_step(0, 0, True, False)
            act_step(1, 1, False, False)
            with act.Fori(0, LOOPS) as i:
                for k in range(2, 2 + NBUF):
                    act_step(i * NBUF + k, k % NBUF, False, False)
            act_step(NSTEP - 2, (NSTEP - 2) % NBUF, False, False)
            act_step(NSTEP - 1, (NSTEP - 1) % NBUF, False, True)
            act.wait_ge(pv_mm, NSTEP * KT)
            act.wait_ge(o_tr, NSTEP - 1)
            act.copy(oT[:, :], bank_o[:, :]).then_inc(oT_ok, 1)
            route_exp(0)

            def take_weights(n):
                act.wait_ge(comb_tr, n + 1)
                act.copy(combT[0:3 * E, n * TB:(n + 1) * TB],
                         bank_w[n].bitcast(BF16)[0:3 * E, 0:TB]).then_inc(combT_ok, 1)

            out_projection(NBLK - 1)
            for n in GROUPS[0]:
                take_weights(n)
            modulate_h2(NBLK - 1)
            route_exp(1)

            def expert_step(e, s, k, p, n):
                q = k % 2
                for c in range(ICH):
                    act.wait_ge(h_mm, s * ICH + c + 1)
                    wait(act, gc_ok, (s - 2) * ICH + c + 1)
                    if c == 0 and n == 0:
                        act.wait_ge(bias_ok, e + 1)
                    act.activation(g_sb[:, q, c, :], bank_h[c], ACT.Gelu,
                                   bias=bias[p][:, c:c + 1]).then_inc(gelu_ok, 1)
                for c in range(ICH):
                    act.wait_ge(gc_ok, s * ICH + c + 1)
                    wait(act, y_mm, s - 1)
                    act.copy(g_hi[:, q, c, :], gc_sb[:, q, c, :]).then_inc(ghi_ok, 1)

            act.wait_ge(in_late, 16 * N_LATE)
            for k, (p, n) in enumerate(BEGINNING):
                expert_step(p, k, k, p, n)
                if k == 3:
                    take_weights(NBLK - 1)
            with act.Fori(1, E // 2) as i:
                for k, (p, n) in enumerate(REGULAR):
                    expert_step(i * 2 + p, i * 2 * NBLK + k, k, p, n)

            for n in range(NBLK):
                act.wait_ge(y_mm, E * NBLK - (NBLK - 1) + n)
                wait(act, y_tr, n - 1)
                act.activation(yT[:, n % 2, :], bank_y[n], ACT.Copy, scale=gb_c[:, n // 2:n // 2 + 1]).then_inc(yT_ok, 1)

        @block.vector
        def _(dve):
            dve.memset(ext[:, :, :], -1.0).then_inc(ext_init, 1)
            dve.memset(combT[:, :], 0.0).then_inc(pad_init, 1)
            dve.memset(b2_parts[:, :, :], 0.0).then_inc(pad_init, 1)
            def statistics(b):
                dve.wait_ge(in_x[b], 16)
                for t in range(b * KT, (b + 1) * KT):
                    dve.bn_stats(stats[:, t, :], x_sb[:, t, :]).then_inc(ln_stat, 1)
                dve.wait_ge(ln_stat, (b + 1) * KT)
                for t in range(b * KT, (b + 1) * KT):
                    dve.bn_aggr(mv[:, t, :], stats[:, t, :]).then_inc(ln_mv, 1)
                dve.wait_ge(ln_mv, (b + 1) * KT)
                r = slice(b * KT, (b + 1) * KT)
                dve.tensor_scalar(veps[:, r], mv[:, r, 1], EPS, None, ALU.add).then_inc(ln_eps, 1)

            def normalise(b):
                dve.wait_ge(ln_rstd, b + 1)
                for t in range(b * KT, (b + 1) * KT):
                    dve.tensor_scalar(xn[:, t, :], x_sb[:, t, :], mv[:, t, 0:1], rstd[:, t:t + 1],
                                      ALU.subtract, ALU.mult).then_inc(ln_done, 1)

            statistics(0)

            dve.wait_ge(silu_exp, 1)
            dve.tensor_scalar(silu_d[:, :], silu_e[:, :], 1.0, None, ALU.add).then_inc(silu_step, 1)
            dve.wait_ge(silu_step, 1)
            dve.reciprocal(silu_r[:, :], silu_d[:, :]).then_inc(silu_step, 1)
            dve.wait_ge(silu_step, 2)
            dve.tensor_tensor(silu_c[:, :], silu_r[:, :], cT_sb[:, :], ALU.mult).then_inc(silu_step, 1)
            dve.wait_ge(silu_step, 3)
            dve.wait_ge(const_ok, 2)
            for b in range(B):
                dve.tensor_scalar(silu_w[:, b, :], ones_w[:, :], silu_c[:, b:b + 1], None, ALU.mult).then_inc(silu_wide, 1)

            normalise(0)

            dve.wait_ge(mod_mm, 1)
            dve.tensor_copy(mod[:, :, :], bank_s[0][:, 0:6 * B].rearrange("p (j b) -> p j b", b=B)).then_inc(mod_ok, 1)
            dve.wait_ge(mod_ok, 1)
            for j in (1, 4):
                dve.tensor_scalar(mod[:, j, :], mod[:, j, :], 1.0, None, ALU.add).then_inc(mod_ok, 1)


            def gates():
                dve.wait_ge(mod_ok, 4)
                for base, raw, s2, mg, gate in ((4, raw_a[:, :, :], sgn[:, :, :], mag[:, :, :], ga_b[:, :, :]),
                                                (8, mod[:, 5, :], gsgn[:, :], gmag[:, :], gb_c[:, :])):
                    dve.tensor_scalar(s2, raw, 0.0, 2.0, ALU.is_ge, ALU.mult).then_inc(mod_ok, 1)
                    dve.scalar_tensor_tensor(out=mg, in0=raw, scalar=-1.0, in1=raw, op0=ALU.mult, op1=ALU.max).then_inc(mod_ok, 1)
                    dve.wait_ge(mod_ok, base + 2)
                    dve.tensor_scalar(mg, mg, 0.25, None, ALU.max).then_inc(mod_ok, 1)
                    dve.wait_ge(mod_ok, base + 3)
                    dve.scalar_tensor_tensor(out=gate, in0=s2, scalar=-1.0, in1=mg, op0=ALU.add, op1=ALU.mult).then_inc(mod_ok, 1)

            def rope(n):
                half = slice((n % 2) * TB, (n % 2 + 1) * TB)
                for w in range(2):
                    k = 2 * n + w
                    wait(dve, rope_sum, k - 1)
                    dve.wait_ge(qk_mm, 2 * k + 1)
                    dve.scalar_tensor_tensor(out=rope_a[:, w, :], in0=bank_m[w][:, 0:TB], scalar=bqk_sb[:, 2 * w:2 * w + 1],
                                             in1=cos_sb[:, half], op0=ALU.add, op1=ALU.mult).then_inc(rope_half, 1)
                    dve.wait_ge(qk_mm, 2 * k + 2)
                    dve.scalar_tensor_tensor(out=rope_b[:, w, :], in0=bank_m[w][:, TB:2 * TB],
                                             scalar=bqk_sb[:, 2 * w + 1:2 * w + 2],
                                             in1=sin_sb[:, half], op0=ALU.add, op1=ALU.mult).then_inc(rope_half, 1)
                    dve.wait_ge(rope_half, 2 * k + 2)
                    wait(dve, part_hi, k - 3)
                    wait(dve, part_rest, k - 3)
                    dve.tensor_tensor(roped[:, n % 2, w, :], rope_a[:, w, :], rope_b[:, w, :], ALU.add).then_inc(rope_sum, 1)

            def value_bias(n):
                dve.wait_ge(v_mm, n + 1)
                dve.tensor_tensor(v_all[:, n * BT:(n + 1) * BT, :], bank_x[:, :].rearrange("p (t c) -> p t c", t=BT),
                                  bv_sb[:, :].unsqueeze(1).broadcast_to([P, BT, C]), ALU.add).then_inc(v_ok, 1)

            statistics(1)
            normalise(1)
            dve.wait_ge(in_proj, 16 * N_PROJ)
            dve.wait_ge(in_rope, 32)
            rope(0)
            rope(1)
            value_bias(0)
            value_bias(1)
            dve.wait_ge(mod_mm, 2)
            dve.tensor_copy(raw_a[:, :, :], bank_s[1][:, 0:B * C].rearrange("p (b c) -> p b c", b=B)).then_inc(mod_ok, 1)
            rope(2)
            rope(3)
            value_bias(2)
            value_bias(3)

            def maxima(m, q, r):
                dve.wait_ge(max_mm, m * MAXU + r + 1)
                wait(dve, shift_lo, (m - NBUF) * HG + r // BT + 1)
                dve.tensor_reduce(neg_max[q][:, r:r + 1], bank_m[r % 2][:, :], AX.X, ALU.max,
                                  negate=True).then_inc(max_ok, 1)
                if r % BT == BT - 1:
                    hh = r // BT
                    cols = slice(hh * BT, (hh + 1) * BT)
                    dve.wait_ge(max_ok, m * MAXU + r + 1)
                    wait(dve, shift_tr, (m - NBUF) * HG + hh + 1)
                    dve.tensor_copy(shift_parts[q][:, cols, 0], neg_max[q][:, cols]).then_inc(shift_hi, 1)
                    dve.wait_ge(shift_hi, m * HG + hh + 1)
                    dve.tensor_tensor(shift_parts[q][:, cols, 1], neg_max[q][:, cols], shift_parts[q][:, cols, 0],
                                      ALU.subtract).then_inc(shift_lo, 1)

            def divide(n, where):
                dve.wait_ge(o_tr, n + 1)
                wait(dve, attn_ok, n)
                o4 = bank_x[:, :].rearrange("p (t h w) -> p t h w", t=BT, h=HG)
                dve.reciprocal(rden[:, :].rearrange("p (t h) -> p t h", t=BT), o4[:, :, :, D]).then_inc(rden_ok, 1)
                dve.wait_ge(rden_ok, n + 1)
                dve.tensor_tensor(where, o4[:, :, :, 0:D],
                                  rden[:, :].rearrange("p (t h) -> p t h", t=BT).unsqueeze(3).broadcast_to([P, BT, HG, D]),
                                  ALU.mult).then_inc(attn_ok, 1)

            attn_g = attn[:, :, :].rearrange("p (n t) c -> p n t c", n=NBLK)

            def attn_at(n):
                return attn_g[:, bass.ds((n & (NSTEP - NG)) >> 2, 1), :, bass.ds((n & (NG - 1)) * (HG * D), HG * D)]\
                    .rearrange("p n t (h d) -> p (n t) h d", h=HG)

            def dve_step(n, p, first):
                for r in range(MAXU):
                    maxima(n + 1, (p + 1) % NBUF, r)
                    if r == 3 and not first:
                        divide(n - 1, attn_at(n - 1))

            def residual(gi):
                tiles = range(GROUPS[gi][0] * BT, (GROUPS[gi][-1] + 1) * BT)
                for n in GROUPS[gi]:
                    dve.wait_ge(wo_mm, n + 1)
                    dve.wait_ge(xbias_ok, B)
                    b = slice(n * BT, (n + 1) * BT)
                    dve.tensor_tensor(x1[:, b, :], bank_w[n].rearrange("p (t c) -> p t c", t=BT), x_sb[:, b, :],
                                      ALU.add).then_inc(x1_ok, 1)
                for n in GROUPS[gi]:
                    dve.wait_ge(x1_ok, n + 1)
                    for t in range(n * BT, (n + 1) * BT):
                        dve.bn_stats(stats[:, t, :], x1[:, t, :]).then_inc(st2, 1)
                for t in tiles:
                    dve.wait_ge(st2, t + 1)
                    dve.bn_aggr(mv[:, t, :], stats[:, t, :]).then_inc(mv2, 1)
                r = slice(tiles[0], tiles[-1] + 1)
                dve.wait_ge(mv2, tiles[-1] + 1)
                dve.tensor_scalar(veps[:, r], mv[:, r, 1], EPS, None, ALU.add).then_inc(eps2, 1)

            def normalise2(gi):
                dve.wait_ge(rstd2, gi + 1)
                for t in range(GROUPS[gi][0] * BT, (GROUPS[gi][-1] + 1) * BT):
                    dve.tensor_scalar(xn[:, t, :], x1[:, t, :], mv[:, t, 0:1], rstd[:, t:t + 1],
                                      ALU.subtract, ALU.mult).then_inc(xn2, 1)

            def low_half(n):
                dve.wait_ge(h2hi_ok, n + 1)
                cols = slice(n * TB, (n + 1) * TB)
                dve.tensor_tensor(h2_lo[:, cols], h2f[:, n, :], h2_hi[:, cols].bitcast(F32), ALU.subtract).then_inc(h2lo_ok, 1)

            def route(gi):
                tiles = range(GROUPS[gi][0] * BT, (GROUPS[gi][-1] + 1) * BT)
                count = len(tiles)
                r = slice(tiles[0], tiles[-1] + 1)
                for n in GROUPS[gi]:
                    b = slice(n * BT, (n + 1) * BT)
                    dve.wait_ge(route_mm, n + 1)
                    dve.wait_ge(in_consts, 16 * N_CONST)
                    dve.tensor_tensor(logit[:, b, :], bank_w[n][:, 0:BT * E].rearrange("p (t e) -> p t e", t=BT),
                                      rb_sb[:, :].unsqueeze(1).broadcast_to([P, BT, E]), ALU.add).then_inc(logit_ok, 1)
                dve.wait_ge(logit_ok, GROUPS[gi][-1] + 1)
                dve.tensor_reduce(neg_lmax[:, r], logit[:, r, :], AX.X, ALU.max, negate=True).then_inc(lmax_ok, 1)
                dve.wait_ge(lmax_ok, 2 * gi + 1)
                dve.tensor_tensor(shifted[:, r, :], logit[:, r, :],
                                  neg_lmax[:, r].unsqueeze(2).broadcast_to([P, count, E]), ALU.add).then_inc(lmax_ok, 1)

            def choose(gi):
                tiles = range(GROUPS[gi][0] * BT, (GROUPS[gi][-1] + 1) * BT)
                count, r, base = len(tiles), slice(tiles[0], tiles[-1] + 1), TOP_BASE[gi]
                dve.wait_ge(rexp_ok, gi + 1)
                for t in tiles:
                    dve.max(top8[:, t, :], ext[:, t, :]).then_inc(top_ok, 1)
                dve.wait_ge(top_ok, base + count)
                dve.memset(top8[:, r, TOPK:8], -1.0).then_inc(top_ok, 1)
                dve.wait_ge(top_ok, base + count + 1)
                for t in tiles:
                    dve.match_replace(marked[:, t, :], top8[:, t, :], ext[:, t, :], -2.0).then_inc(top_ok, 1)

            def weigh(gi):
                tiles = range(GROUPS[gi][0] * BT, (GROUPS[gi][-1] + 1) * BT)
                count, r, base = len(tiles), slice(tiles[0], tiles[-1] + 1), TOP_BASE[gi]
                dve.wait_ge(top_ok, base + 2 * count + 1)
                dve.scalar_tensor_tensor(out=chosen[:, r, :], in0=marked[:, r, 0:E], scalar=-2.0, in1=ext[:, r, 0:E],
                                         op0=ALU.is_equal, op1=ALU.mult).then_inc(top_ok, 1)
                dve.wait_ge(top_ok, base + 2 * count + 2)
                dve.tensor_reduce(csum[:, r], chosen[:, r, :], AX.X, ALU.add).then_inc(top_ok, 1)
                dve.wait_ge(top_ok, base + 2 * count + 3)
                dve.reciprocal(crec[:, r], csum[:, r]).then_inc(top_ok, 1)
                dve.wait_ge(top_ok, base + 2 * count + 4)
                dve.tensor_tensor(comb[:, r, :], chosen[:, r, :], crec[:, r].unsqueeze(2).broadcast_to([P, count, E]),
                                  ALU.mult).then_inc(comb_ok, 1)
                dve.wait_ge(comb_ok, gi + 1)
                dve.tensor_copy(comb_parts[:, r, 0, :], comb[:, r, :]).then_inc(top_ok, 1)
                dve.wait_ge(top_ok, base + 2 * count + 5)
                dve.tensor_tensor(comb_r[:, r, :], comb[:, r, :], comb_parts[:, r, 0, :], ALU.subtract).then_inc(top_ok, 1)
                dve.wait_ge(top_ok, base + 2 * count + 6)
                dve.tensor_copy(comb_parts[:, r, 1, :], comb_r[:, r, :]).then_inc(top_ok, 1)
                dve.wait_ge(top_ok, base + 2 * count + 7)
                dve.tensor_tensor(comb_parts[:, r, 2, :], comb_r[:, r, :], comb_parts[:, r, 1, :], ALU.subtract).then_inc(top_ok, 1)

            for r in range(MAXU):
                maxima(0, 0, r)
            dve_step(0, 0, True)
            dve_step(1, 1, False)
            gates()
            with dve.Fori(0, LOOPS) as i:
                for k in range(2, 2 + NBUF):
                    dve_step(i * NBUF + k, k % NBUF, False)
            dve_step(NSTEP - 2, (NSTEP - 2) % NBUF, False)
            dve.wait_ge(in_late, 16 * N_LATE)
            dve.wait_ge(pad_init, 2)
            rows = slice(0, 3 * E)
            dve.tensor_copy(b2_parts[rows, 0, :], b2_sb[rows, :]).then_inc(b2_step, 1)
            dve.wait_ge(b2_step, 1)
            dve.tensor_tensor(b2_r[rows, :], b2_sb[rows, :], b2_parts[rows, 0, :], ALU.subtract).then_inc(b2_step, 1)
            dve.wait_ge(b2_step, 2)
            dve.tensor_copy(b2_parts[rows, 1, :], b2_r[rows, :]).then_inc(b2_step, 1)
            dve.wait_ge(b2_step, 3)
            dve.tensor_tensor(b2_parts[rows, 2, :], b2_r[rows, :], b2_parts[rows, 1, :], ALU.subtract).then_inc(b2_step, 1)

            for n in GROUPS[0]:
                dve.wait_ge(a_tr, n + 1)
                dve.tensor_copy(attnT[:, n, :], bank_w[n]).then_inc(aT_ok, 1)
            divide(NSTEP - 2, attn_at(NSTEP - 2))
            residual(0)
            normalise2(0)
            for n in GROUPS[0]:
                b = n // 2
                dve.wait_ge(x2_tr, n + 1)
                dve.tensor_scalar(h2f[:, n, :], bank_w[n], mod[:, 4, b:b + 1], mod[:, 3, b:b + 1],
                                  ALU.mult, ALU.add).then_inc(h2_ok, 1)
            for n in GROUPS[0]:
                dve.wait_ge(h2_ok, n + 1)
                dve.tensor_copy(h2_hi[:, n * TB:(n + 1) * TB], h2f[:, n, :]).then_inc(h2hi_ok, 1)
            for n in GROUPS[0]:
                low_half(n)

            route(0)
            divide(NSTEP - 1, attn_at(NSTEP - 1))
            choose(0)
            weigh(0)
            residual(1)
            normalise2(1)
            route(1)

            def expert_step(s, k):
                q = k % 2
                for c in range(ICH):
                    dve.wait_ge(gelu_ok, s * ICH + c + 1)
                    if c == 0:
                        dve.wait_ge(cb_mm, s + 1)
                    wait(dve, glo_ok, (s - 2) * ICH + c + 1)
                    dve.tensor_tensor(gc_sb[:, q, c, :], g_sb[:, q, c, :], bank_c[q], ALU.mult).then_inc(gc_ok, 1)
                for c in range(ICH):
                    dve.wait_ge(ghi_ok, s * ICH + c + 1)
                    wait(dve, y_mm, s - 1)
                    dve.tensor_tensor(g_lo[:, q, c, :], gc_sb[:, q, c, :], g_hi[:, q, c, :].bitcast(F32),
                                      ALU.subtract).then_inc(glo_ok, 1)

            for k in range(2 * NBLK):
                expert_step(k, k)
                if k == 0:
                    low_half(NBLK - 1)
                if k == 1:
                    choose(1)
                if k == 2:
                    weigh(1)
            with dve.Fori(1, E // 2) as i:
                for k in range(2 * NBLK):
                    expert_step(i * 2 * NBLK + k, k)

            for n in range(NBLK):
                dve.wait_ge(y_tr, n + 1)
                r = slice(n * BT, (n + 1) * BT)
                dve.tensor_tensor(x1[:, r, :], bank_y[n].rearrange("p (t c) -> p t c", t=BT), x1[:, r, :],
                                  ALU.add).then_inc(out_ok, 1)

        @block.tensor
        def _(pe):
            pe.wait_ge(in_mod, 16 * N_MODIN)
            pe.wait_ge(silu_step, 3)
            for j in range(6):
                mm = pe.matmul(bank_s[0][:, j * B:(j + 1) * B], wmod_sb[:, j, :], silu_c[:, :], start=True, stop=True)
            mm.then_inc(mod_mm, 1)

            def transpose_x(n):
                pe.wait_ge(ln_done, (n + 1) * BT)
                wait(pe, hT_ok, n)
                for t in range(BT):
                    mm = pe.transpose(bank_o[:, t * P:(t + 1) * P], xn[:, n * BT + t, :], id_f[:, :])
                mm.then_inc(xT_mm, 1)

            def project(n):
                cols = slice(n * TB, (n + 1) * TB)
                pe.wait_ge(hT_ok, n + 1)
                for w in range(2):
                    for j in range(2):
                        wait(pe, rope_half, 4 * (n - 1) + 2 * w + j + 1)
                        pe.matmul(bank_m[w][:, j * TB:(j + 1) * TB], wqk_sb[:, 2 * w + j, :], hT[:, cols],
                                  start=True, stop=True).then_inc(qk_mm, 1)

            def project_v(n):
                wait(pe, v_ok, n)
                for t in range(BT):
                    tok = n * TB + t * P
                    mm = pe.matmul(bank_x[:, t * C:(t + 1) * C], hT[:, tok:tok + P], wv_sb[:, :], start=True, stop=True)
                mm.then_inc(v_mm, 1)

            pe.wait_ge(in_proj, 16 * N_PROJ)
            transpose_x(0)
            transpose_x(1)
            project(0)
            project(1)
            transpose_x(2)
            transpose_x(3)
            project_v(0)
            project_v(1)
            pe.wait_ge(silu_wide, B)
            for b in range(B):
                mm = pe.matmul(bank_s[1][:, b * C:(b + 1) * C], silu_w[:, b, :], wmod_sb[:, 2, :], start=True, stop=True)
            mm.then_inc(mod_mm, 1)
            project(2)
            project(3)
            project_v(2)
            project_v(3)

            def max_half(m, q, r, half):
                hh, t = r // BT, r % BT
                if half == 0:
                    wait(pe, max_ok, m * MAXU + r - 1)
                mm = pe.matmul(bank_m[r % 2][:, half * TB:(half + 1) * TB], Qs[q][:, hh, t * P:(t + 1) * P],
                               Ks[q][:, hh, half * TB:(half + 1) * TB], start=True, stop=True)
                if half == 1:
                    mm.then_inc(max_mm, 1)

            def turn_shift(m, q, hh):
                pe.wait_ge(shift_lo, m * HG + hh + 1)
                wait(pe, shift_ok, m * HG + hh)
                for t in range(BT):
                    mm = pe.transpose(shift_psum[:, t * P:(t + 1) * P], shift_parts[q][:, hh * BT + t, :], id_b[:, :])
                mm.then_inc(shift_tr, 1)

            def scores(n, p, kt, hh, last):
                u = kt * HG + hh
                banks = bank_e_last if last else bank_e
                if last and u == len(bank_e):
                    pe.wait_ge(max_ok, NSTEP * MAXU)
                else:
                    back = len(bank_e) if u < len(bank_e) else len(banks)
                    wait(pe, exp_ok, n * UNITS + (u + 1 - back))
                if kt == 0:
                    pe.wait_ge(shift_ok, n * HG + hh + 1)
                pe.matmul(banks[u % len(banks)], Ks[p][:, hh, kt * P:(kt + 1) * P], Qs[p][:, hh, :],
                          start=True, stop=True).then_inc(score_mm, 1)

            def products(n, p, kt):
                pe.wait_ge(exp_ok, n * UNITS + (kt + 1) * HG)
                if kt == 0:
                    pe.wait_ge(v_staged, n + 1)
                    wait(pe, oT_ok, n)
                for hh in range(HG):
                    mm = pe.matmul(bank_o[hh * VW:(hh + 1) * VW, :], Vs[p][:, kt, hh, :],
                                   prob[:, (kt * HG + hh) % RING, :], start=(kt == 0), stop=(kt == KT - 1))
                mm.then_inc(pv_mm, 1)

            def turn_sums(n):
                pe.wait_ge(oT_ok, n + 1)
                wait(pe, attn_ok, n)
                for t in range(BT):
                    mm = pe.transpose(bank_x[:, t * P:(t + 1) * P], oT[:, t * P:(t + 1) * P], id_f[:, :])
                mm.then_inc(o_tr, 1)

            def turn_attention(n):
                for t in range(BT):
                    mm = pe.transpose(bank_w[n][:, t * P:(t + 1) * P], attn[:, n * BT + t, :], id_f[:, :])
                mm.then_inc(a_tr, 1)

            def out_product(n):
                pe.wait_ge(gate_ok, 2 * B)
                pe.wait_ge(aT_ok, n + 1)
                for t in range(BT):
                    mm = pe.matmul(bank_w[n][:, t * C:(t + 1) * C], attnT[:, n, t * P:(t + 1) * P], wo_g[:, n // 2, :],
                                   start=True, stop=True)
                mm.then_inc(wo_mm, 1)

            def turn_normalised(n):
                pe.wait_ge(xn2, (n + 1) * BT)
                for t in range(BT):
                    mm = pe.transpose(bank_w[n][:, t * P:(t + 1) * P], xn[:, n * BT + t, :], id_f[:, :])
                mm.then_inc(x2_tr, 1)

            def router(n):
                pe.wait_ge(h2_ok, n + 1)
                for t in range(BT):
                    mm = pe.matmul(bank_w[n][:, t * E:(t + 1) * E], h2f[:, n, t * P:(t + 1) * P], rw_sb[:, :],
                                   start=True, stop=True)
                mm.then_inc(route_mm, 1)

            def turn_weights(n):
                pe.wait_ge(top_ok, TOP_BASE[1 if n in GROUPS[0] else 2])
                for t in range(BT):
                    mm = pe.transpose(bank_w[n].bitcast(BF16)[0:3 * E, t * P:(t + 1) * P],
                                      comb_parts[:, n * BT + t, :, :].rearrange("p a e -> p (a e)"), id_b[:, :])
                mm.then_inc(comb_tr, 1)

            def pe_step(n, p, turn, first, last):
                m, q = n + 1, (p + 1) % NBUF
                for kt in range(KT):
                    scores(n, p, kt, 0, last)
                    if not last:
                        if kt == 0:
                            pe.wait_ge(staged[q], (turn + 1) * 48)
                            max_half(m, q, 0, 0)
                        max_half(m, q, 2 * kt, 1)
                        max_half(m, q, 2 * kt + 1, 0)
                    scores(n, p, kt, 1, last)
                    if not last:
                        max_half(m, q, 2 * kt + 1, 1)
                    scores(n, p, kt, 2, last)
                    if last and kt > 0:
                        scores(n, p, kt, 3, last)
                    if kt > 0:
                        products(n, p, kt - 1)
                    elif not first:
                        turn_shift(n, p, HG - 1)
                        products(n - 1, (p - 1) % NBUF, KT - 1)
                    if kt == 0 or not last:
                        scores(n, p, kt, 3, last)
                    if not last and kt + 1 < KT:
                        max_half(m, q, 2 * kt + 2, 0)
                    if kt == 1 and not first:
                        turn_sums(n - 1)
                    if kt in SHIFT_AT and not last:
                        if kt == SHIFT_AT[0]:
                            wait(pe, attn_ok, n)
                        turn_shift(m, q, SHIFT_AT.index(kt))
                    if last and kt == 0:
                        for b in GROUPS[0]:
                            turn_attention(b)
                    if last and kt == 1:
                        for b in GROUPS[0]:
                            out_product(b)
                    if last and kt == 7:
                        router(0)
                    if last and kt == 5:
                        for b in GROUPS[0]:
                            turn_normalised(b)

            pe.wait_ge(rope_half, 4 * NBLK)
            pe.wait_ge(v_ok, NBLK)
            pe.wait_ge(hT_ok, NBLK)
            pe.wait_ge(mod_ok, 4)
            pe.wait_ge(in_consts, 16 * N_CONST)
            pe.wait_ge(staged[0], 48)
            for r in range(MAXU):
                max_half(0, 0, r, 0)
                max_half(0, 0, r, 1)
                if r % BT == BT - 1 and r > BT:
                    turn_shift(0, 0, r // BT - 1)
            turn_shift(0, 0, HG - 1)
            pe_step(0, 0, 0, True, False)
            pe_step(1, 1, 0, False, False)
            with pe.Fori(0, LOOPS) as i:
                for k in range(2, 2 + NBUF):
                    pe_step(i * NBUF + k, k % NBUF, i + (k + 1) // NBUF, False, False)
            pe_step(NSTEP - 2, (NSTEP - 2) % NBUF, (NSTEP - 1) // NBUF, False, False)
            pe_step(NSTEP - 1, (NSTEP - 1) % NBUF, None, False, True)
            products(NSTEP - 1, (NSTEP - 1) % NBUF, KT - 1)
            router(1)
            router(2)
            turn_sums(NSTEP - 1)
            pe.wait_ge(attn_ok, NSTEP)
            turn_attention(NBLK - 1)
            out_product(NBLK - 1)
            for n in GROUPS[0]:
                turn_weights(n)

            def add_bias(n, begin):
                pe.wait_ge(combT_ok, n + 1)
                for i in range(3):
                    pe.matmul(bank_y[n], b2_parts[:, i, :], combT[:, n * TB:(n + 1) * TB],
                              start=(begin and i == 0), stop=False,
                              skip_group_check=True)

            def expert_hidden(e, s, k, p, n):
                q = k % 2
                cols = slice(n * TB, (n + 1) * TB)
                if n == 0:
                    pe.wait_ge(w_lo_ok, e * 2 + 1)
                wait(pe, gc_ok, (s - 1) * ICH)
                pe.matmul(bank_c[q], select_sb[:, bass.ds(e, 1), :].rearrange("k e m -> k (e m)"), combT[:, cols],
                          start=True, stop=True).then_inc(cb_mm, 1)
                for c in range(ICH):
                    part = slice(c * P, (c + 1) * P)
                    wait(pe, gelu_ok, (s - 1) * ICH + c + 1)
                    pe.matmul(bank_h[c], w_hi[p][:, 0, part], h2_hi[:, cols], start=True, stop=False)
                    pe.matmul(bank_h[c], w_hi[p][:, 0, part], h2_lo[:, cols], start=False, stop=False)
                    pe.matmul(bank_h[c], w_lo[p][:, 0, part], h2_hi[:, cols], start=False, stop=True).then_inc(h_mm, 1)

            def expert_sum(e, s, k, p, n, begin=False):
                q = k % 2
                if n == 0:
                    pe.wait_ge(w_lo_ok, e * 2 + 2)
                for c in range(ICH):
                    part = slice(c * C, (c + 1) * C)
                    pe.wait_ge(ghi_ok, s * ICH + c + 1)
                    pe.matmul(bank_y[n], w_hi[p][:, 1, part], g_hi[:, q, c, :], start=(begin and c == 0), stop=False, skip_group_check=True)
                    pe.matmul(bank_y[n], w_lo[p][:, 1, part], g_hi[:, q, c, :], start=False, stop=False, skip_group_check=True)
                    pe.wait_ge(glo_ok, s * ICH + c + 1)
                    mm = pe.matmul(bank_y[n], w_hi[p][:, 1, part], g_lo[:, q, c, :], start=False, stop=True, skip_group_check=True)
                mm.then_inc(y_mm, 1)

            LAST = 2 * NBLK - 1
            pe.wait_ge(h2lo_ok, NBLK - 1)
            pe.wait_ge(combT_ok, NBLK - 1)
            pe.wait_ge(b2_step, 4)
            add_bias(0, True)
            add_bias(1, True)
            turn_normalised(NBLK - 1)
            add_bias(2, True)
            router(NBLK - 1)
            expert_hidden(0, 0, 0, 0, 0)
            for k in range(LAST):
                p, n = BEGINNING[k + 1]
                if k + 1 == BEGINNING.index((0, NBLK - 1)):
                    pe.wait_ge(h2lo_ok, NBLK)
                    pe.wait_ge(combT_ok, NBLK)
                expert_hidden(p, k + 1, k + 1, p, n)
                expert_sum(BEGINNING[k][0], k, k, *BEGINNING[k], begin=BEGINNING[k] == (0, NBLK - 1))
                if k == 3:
                    turn_weights(NBLK - 1)
            add_bias(NBLK - 1, False)
            with pe.Fori(1, E // 2) as i:
                for k in range(-1, LAST):
                    p, n = REGULAR[k + 1]
                    expert_hidden(i * 2 + p, i * 2 * NBLK + k + 1, k + 1, p, n)
                    p, n = REGULAR[k]
                    expert_sum(i * 2 + (p if k >= 0 else -1), i * 2 * NBLK + k, k % (2 * NBLK), p, n)

            for n in range(NBLK):
                if n == 1:
                    expert_sum(E - 1, E * NBLK - 1, LAST, 1, NBLK - 1)
                pe.wait_ge(yT_ok, n + 1)
                for t in range(BT):
                    mm = pe.transpose(bank_y[n][:, t * P:(t + 1) * P], yT[:, n % 2, t * P:(t + 1) * P], id_f[:, :])
                mm.then_inc(y_tr, 1)


def kernel(L0_attn_x, L0_attn_Wq, L0_attn_bq, L0_attn_Wk, L0_attn_bk, L0_attn_Wv, L0_attn_bv, L0_attn_Wo, L0_attn_bo,
           L0_ffn_router_w, L0_ffn_router_b, L0_ffn_w1, L0_ffn_b1, L0_ffn_w2, L0_ffn_b2, L0_c, L0_wmod):
    import numpy as np
    import concourse.bacc as bacc
    from concourse.bass_utils import run_bass_kernel_spmd

    f32 = np.float32
    swap = np.arange(H * D).reshape(H, 2, D // 2)[:, ::-1].reshape(-1)
    theta = f32(10000.0) ** (-np.arange(D // 2, dtype=f32) / f32(D // 2))
    angle = np.arange(T, dtype=f32)[:, None] * theta[None, :]
    cos = np.tile(np.cos(angle).T, (2 * H, 1)).astype(f32)
    sin = np.tile(np.concatenate([-np.sin(angle).T, np.sin(angle).T]), (H, 1)).astype(f32)
    row = np.arange(P)
    select = ((row[:, None] % E == np.arange(E)[None, :]) & (row[:, None] < 3 * E))
    select = np.repeat(select[:, :, None], P, axis=2).reshape(P, E * P)
    bf16 = mybir.dt.np(BF16)
    wq, wk = np.asarray(L0_attn_Wq), np.asarray(L0_attn_Wk)
    bq, bk = np.asarray(L0_attn_bq), np.asarray(L0_attn_bk)
    arrays = {
        "x": np.asarray(L0_attn_x),
        "wqkT": np.stack([wq.T, wq[swap].T, wk.T, wk[swap].T]),
        "bqk": np.stack([bq, bq[swap], bk, bk[swap]], axis=1),
        "wvT": np.asarray(L0_attn_Wv).T,
        "bv": np.asarray(L0_attn_bv),
        "woT": np.asarray(L0_attn_Wo).T,
        "bo": np.asarray(L0_attn_bo),
        "router_w": np.asarray(L0_ffn_router_w),
        "router_b": np.asarray(L0_ffn_router_b),
        "w1": np.asarray(L0_ffn_w1),
        "b1T": np.asarray(L0_ffn_b1).reshape(E * ICH, P).T,
        "w2": np.asarray(L0_ffn_w2),
        "b2": np.asarray(L0_ffn_b2),
        "cT": np.asarray(L0_c).T,
        "wmod": np.asarray(L0_wmod),
        "cos": cos,
        "sin": sin,
        "ident": np.eye(P, dtype=f32),
        "identb": np.eye(P).astype(bf16),
        "select": select.astype(bf16),
    }
    nc = bacc.Bacc("TRN2", target_bir_lowering=False, num_devices=1)
    feeds, args = {}, []
    for name, a in arrays.items():
        a = np.ascontiguousarray(a)
        feeds[f"in_{name}"] = a
        args.append(nc.dram_tensor(f"in_{name}", a.shape, mybir.dt.from_np(a.dtype), kind="ExternalInput").ap())
    args.append(nc.dram_tensor("out_dram", (B, T, C), F32, kind="ExternalOutput").ap())
    block_program(nc, *args)
    r = run_bass_kernel_spmd(nc, [feeds], core_ids=[0])
    return r.results[0]["out_dram"]
```
